# Optimizing a Trainium2 kernel written in Bass

```python
import numpy as np
import jax
import jax.numpy as jnp

def _softmax(x, axis=-1):
    return jax.nn.softmax(x, axis=axis)

def _gelu(x):
    return jax.nn.gelu(x, approximate=True)

def _silu(x):
    return jax.nn.silu(x)

def _sigmoid(x):
    return jax.nn.sigmoid(x)

def _layernorm(x, axis=-1, eps=1e-05):
    m = jnp.mean(x, axis=axis, keepdims=True)
    v = jnp.var(x, axis=axis, keepdims=True)
    return (x - m) / jnp.sqrt(v + eps)

def _scatter_add(tgt, idx, src, axis=0):
    return tgt.at[idx].add(src)

def _segment_sum(src, seg, n):
    return jax.ops.segment_sum(src, seg, n)
kernel_name = 'mk_seq_preln_d2_jaxref_r8_ab8d63'

def setup_inputs(seed: int=0):
    np.random.seed(seed)
    _w = jnp.asarray

    def _L0_attn_setup():
        import jax, jax.numpy as jnp
        import numpy as np
        EMBED_DIM = 256
        NUM_HEADS = 32
        HEAD_DIM = EMBED_DIM // NUM_HEADS
        BATCH = 2
        SEQ_LEN = 256
        key = jax.random.key(seed)
        ks = jax.random.split(key, 5)
        scale = 1.0 / np.sqrt(EMBED_DIM)
        x = jax.random.normal(ks[0], (BATCH, SEQ_LEN, EMBED_DIM), dtype=jnp.float32)
        Wq = jax.random.normal(ks[1], (EMBED_DIM, EMBED_DIM), dtype=jnp.float32) * scale
        Wk = jax.random.normal(ks[2], (EMBED_DIM, EMBED_DIM), dtype=jnp.float32) * scale
        Wv = jax.random.normal(ks[3], (EMBED_DIM, EMBED_DIM), dtype=jnp.float32) * scale
        Wo = jax.random.normal(ks[4], (EMBED_DIM, EMBED_DIM), dtype=jnp.float32) * scale
        return {'x': x, 'Wq': Wq, 'Wk': Wk, 'Wv': Wv, 'Wo': Wo}
    _L0_attn_in = _L0_attn_setup()

    def _L0_ffn_setup():
        import jax, jax.numpy as jnp
        import numpy as np
        HIDDEN = 256
        INTER = 1024
        BATCH, LOCAL_SEQ = (2, 512)
        key = jax.random.key(seed)
        k1, k2, k3 = jax.random.split(key, 3)
        h_shard = jax.random.normal(k1, (BATCH, LOCAL_SEQ, HIDDEN), dtype=jnp.float32)
        w_gate_up = jax.random.normal(k2, (2 * INTER, HIDDEN), dtype=jnp.float32) * 0.02
        w_down = jax.random.normal(k3, (HIDDEN, INTER), dtype=jnp.float32) * 0.02
        return {'h_shard': h_shard, 'w_gate_up': w_gate_up, 'w_down': w_down}
    _L0_ffn_in = _L0_ffn_setup()

    def _L1_attn_setup():
        import jax, jax.numpy as jnp
        import numpy as np
        N_HEAD = 32
        N_KV_HEAD = 8
        HEAD_DIM = 64
        N_EMBD = 256
        B, T = (2, 256)
        ROPE_BASE = 10000.0

        def _rope_cos_sin(T, head_dim, dtype):
            pos = jnp.arange(T, dtype=jnp.float32)
            dim_arr = jnp.arange(0, head_dim, 2, dtype=jnp.float32)
            freqs = ROPE_BASE ** (-dim_arr / head_dim)
            theta = jnp.outer(pos, freqs)
            cos = jnp.concatenate([jnp.cos(theta), jnp.cos(theta)], axis=-1)
            sin = jnp.concatenate([jnp.sin(theta), jnp.sin(theta)], axis=-1)
            return (cos[None, :, None, :].astype(dtype), sin[None, :, None, :].astype(dtype))

        def _rotate_half(v):
            h = v.shape[-1] // 2
            return jnp.concatenate([-v[..., h:], v[..., :h]], axis=-1)
        key = jax.random.key(seed)
        kx, kq, kk, kv, ko = jax.random.split(key, 5)
        s = 1.0 / np.sqrt(N_EMBD)
        return {'x': jax.random.normal(kx, (B, T, N_EMBD), dtype=jnp.float32), 'wq': jax.random.normal(kq, (N_EMBD, N_HEAD * HEAD_DIM), dtype=jnp.float32) * s, 'wk': jax.random.normal(kk, (N_EMBD, N_KV_HEAD * HEAD_DIM), dtype=jnp.float32) * s, 'wv': jax.random.normal(kv, (N_EMBD, N_KV_HEAD * HEAD_DIM), dtype=jnp.float32) * s, 'wo': jax.random.normal(ko, (N_HEAD * HEAD_DIM, N_EMBD), dtype=jnp.float32) * s}
    _L1_attn_in = _L1_attn_setup()

    def _L1_ffn_setup():
        import jax, jax.numpy as jnp
        import numpy as np
        EPS = 1e-06
        Q_B = 128.0

        def layer_norm(x):
            mean = jnp.mean(x, axis=-1, keepdims=True)
            var = jnp.var(x, axis=-1, keepdims=True)
            return (x - mean) / jnp.sqrt(var + EPS)

        def absmax_quant(x):
            gamma = jnp.max(jnp.abs(x), axis=-1, keepdims=True)
            x_hat = jnp.clip(x * Q_B / gamma, -Q_B + EPS, Q_B - EPS)
            return x_hat * gamma / Q_B

        def ternarize_weights(w):
            gamma = jnp.mean(jnp.abs(w))
            return jnp.sign(jnp.round(w / (gamma + EPS))) * gamma

        def bitlinear(x, w):
            xn = layer_norm(x)
            x_hat = xn + jax.lax.stop_gradient(absmax_quant(xn) - xn)
            w_hat = w + jax.lax.stop_gradient(ternarize_weights(w) - w)
            return jnp.einsum('bsd,od->bso', x_hat, w_hat)
        key = jax.random.key(seed)
        k1, k2, k3 = jax.random.split(key, 3)
        B, S, D = (4, 256, 256)
        x = jax.random.normal(k1, (B, S, D), dtype=jnp.float32)
        w_fc = jax.random.normal(k2, (4 * D, D), dtype=jnp.float32) / np.sqrt(D)
        w_proj = jax.random.normal(k3, (D, 4 * D), dtype=jnp.float32) / np.sqrt(4 * D)
        return {'x': x, 'w_fc': w_fc, 'w_proj': w_proj}
    _L1_ffn_in = _L1_ffn_setup()
    _d = {'L0_attn_x': _L0_attn_in['x'], 'L0_attn_Wq': _L0_attn_in['Wq'], 'L0_attn_Wk': _L0_attn_in['Wk'], 'L0_attn_Wv': _L0_attn_in['Wv'], 'L0_attn_Wo': _L0_attn_in['Wo'], 'L0_ffn_w_gate_up': _L0_ffn_in['w_gate_up'], 'L0_ffn_w_down': _L0_ffn_in['w_down'], 'L1_attn_wq': _L1_attn_in['wq'], 'L1_attn_wk': _L1_attn_in['wk'], 'L1_attn_wv': _L1_attn_in['wv'], 'L1_attn_wo': _L1_attn_in['wo'], 'L1_ffn_w_fc': _L1_ffn_in['w_fc'], 'L1_ffn_w_proj': _L1_ffn_in['w_proj']}
    _x0 = _d['L0_attn_x']
    _d['L0_attn_x'] = jax.random.normal(jax.random.fold_in(jax.random.key(seed), 1), (1, 1024, 256), dtype=_x0.dtype)
    del _x0
    return _d

def reference(L0_attn_x, L0_attn_Wq, L0_attn_Wk, L0_attn_Wv, L0_attn_Wo, L0_ffn_w_gate_up, L0_ffn_w_down, L1_attn_wq, L1_attn_wk, L1_attn_wv, L1_attn_wo, L1_ffn_w_fc, L1_ffn_w_proj):

    def _L0_attn_ref(x, Wq, Wk, Wv, Wo):
        import jax, jax.numpy as jnp
        import numpy as np
        EMBED_DIM = 256
        NUM_HEADS = 32
        HEAD_DIM = EMBED_DIM // NUM_HEADS
        BATCH = 2
        SEQ_LEN = 256
        q = jnp.einsum('bse,ef->bsf', x, Wq)
        k = jnp.einsum('bse,ef->bsf', x, Wk)
        v = jnp.einsum('bse,ef->bsf', x, Wv)
        qT = jnp.swapaxes(q, 1, 2)
        kT = jnp.swapaxes(k, 1, 2)
        vT = jnp.swapaxes(v, 1, 2)
        attn_scores = jnp.einsum('bes,bfs->bef', qT, kT) / np.sqrt(HEAD_DIM)
        attn_weights = jax.nn.softmax(attn_scores, axis=-1)
        attn_output = jnp.einsum('bef,bfs->bes', attn_weights, vT)
        attn_output = jnp.swapaxes(attn_output, 1, 2)
        return jnp.einsum('bse,ef->bsf', attn_output, Wo)

    def _L0_ffn_ref(h_shard, w_gate_up, w_down):
        import jax, jax.numpy as jnp
        import numpy as np
        HIDDEN = 256
        INTER = 1024
        BATCH, LOCAL_SEQ = (2, 512)
        batch, local_seq, hidden = h_shard.shape
        gate_up = jnp.einsum('bsh,oh->bso', h_shard, w_gate_up)
        gate, up = jnp.split(gate_up, 2, axis=-1)
        h = jax.nn.silu(gate) * up
        out = jnp.einsum('bsi,hi->bsh', h, w_down)
        return out

    def _L1_attn_ref(x, wq, wk, wv, wo):
        import jax, jax.numpy as jnp
        import numpy as np
        N_HEAD = 32
        N_KV_HEAD = 8
        HEAD_DIM = 64
        N_EMBD = 256
        B, T = (2, 256)
        ROPE_BASE = 10000.0

        def _rope_cos_sin(T, head_dim, dtype):
            pos = jnp.arange(T, dtype=jnp.float32)
            dim_arr = jnp.arange(0, head_dim, 2, dtype=jnp.float32)
            freqs = ROPE_BASE ** (-dim_arr / head_dim)
            theta = jnp.outer(pos, freqs)
            cos = jnp.concatenate([jnp.cos(theta), jnp.cos(theta)], axis=-1)
            sin = jnp.concatenate([jnp.sin(theta), jnp.sin(theta)], axis=-1)
            return (cos[None, :, None, :].astype(dtype), sin[None, :, None, :].astype(dtype))

        def _rotate_half(v):
            h = v.shape[-1] // 2
            return jnp.concatenate([-v[..., h:], v[..., :h]], axis=-1)
        Bx, Tx, C = x.shape
        n_rep = N_HEAD // N_KV_HEAD
        xq = (x @ wq).reshape(Bx, Tx, N_HEAD, HEAD_DIM)
        xk = (x @ wk).reshape(Bx, Tx, N_KV_HEAD, HEAD_DIM)
        xv = (x @ wv).reshape(Bx, Tx, N_KV_HEAD, HEAD_DIM)
        cos, sin = _rope_cos_sin(Tx, HEAD_DIM, x.dtype)
        xq = xq * cos + _rotate_half(xq) * sin
        xk = xk * cos + _rotate_half(xk) * sin
        xk = jnp.repeat(xk, n_rep, axis=2)
        xv = jnp.repeat(xv, n_rep, axis=2)
        scale = 1.0 / np.sqrt(HEAD_DIM)
        scores = jnp.einsum('bqhd,bkhd->bhqk', xq, xk) * scale
        causal = jnp.tril(jnp.ones((Tx, Tx), dtype=bool))
        scores = jnp.where(causal[None, None], scores, -jnp.inf)
        probs = jax.nn.softmax(scores, axis=-1)
        out = jnp.einsum('bhqk,bkhd->bqhd', probs, xv).reshape(Bx, Tx, N_HEAD * HEAD_DIM)
        return out @ wo

    def _L1_ffn_ref(x, w_fc, w_proj):
        import jax, jax.numpy as jnp
        import numpy as np
        EPS = 1e-06
        Q_B = 128.0

        def layer_norm(x):
            mean = jnp.mean(x, axis=-1, keepdims=True)
            var = jnp.var(x, axis=-1, keepdims=True)
            return (x - mean) / jnp.sqrt(var + EPS)

        def absmax_quant(x):
            gamma = jnp.max(jnp.abs(x), axis=-1, keepdims=True)
            x_hat = jnp.clip(x * Q_B / gamma, -Q_B + EPS, Q_B - EPS)
            return x_hat * gamma / Q_B

        def ternarize_weights(w):
            gamma = jnp.mean(jnp.abs(w))
            return jnp.sign(jnp.round(w / (gamma + EPS))) * gamma

        def bitlinear(x, w):
            xn = layer_norm(x)
            x_hat = xn + jax.lax.stop_gradient(absmax_quant(xn) - xn)
            w_hat = w + jax.lax.stop_gradient(ternarize_weights(w) - w)
            return jnp.einsum('bsd,od->bso', x_hat, w_hat)
        h = bitlinear(x, w_fc)
        h = jax.nn.gelu(h, approximate=False)
        return bitlinear(h, w_proj)
    x = L0_attn_x
    x = x + _L0_attn_ref(_layernorm(x, axis=-1), L0_attn_Wq, L0_attn_Wk, L0_attn_Wv, L0_attn_Wo)
    x = x + _L0_ffn_ref(_layernorm(x, axis=-1), L0_ffn_w_gate_up, L0_ffn_w_down)
    x = x + _L1_attn_ref(_layernorm(x, axis=-1), L1_attn_wq, L1_attn_wk, L1_attn_wv, L1_attn_wo)
    x = x + _L1_ffn_ref(_layernorm(x, axis=-1), L1_ffn_w_fc, L1_ffn_w_proj)
    return x

_drawn_inputs = setup_inputs


def setup_inputs(seed=0):
    import zlib

    import numpy as np

    out = dict(_drawn_inputs(seed))
    spreads = {}
    factors = {}
    for name, (base, spread) in spreads.items():
        noise = np.random.default_rng([zlib.crc32(name.encode()), seed]).standard_normal(out[name].shape)
        drawn = base * np.exp(spread * noise) if base else spread * noise
        out[name] = jnp.asarray(drawn.astype(out[name].dtype))
    for name, factor in factors.items():
        out[name] = (out[name] * factor).astype(out[name].dtype)
    return out
```

```python
from contextlib import ExitStack

import concourse.bass as bass
from concourse import mybir

F32 = mybir.dt.float32
F32R = mybir.dt.float32r
F16 = mybir.dt.float16
BF16 = mybir.dt.bfloat16
ALU = mybir.AluOpType
ACT = mybir.ActivationFunctionType
AX = mybir.AxisListType

P = 128
BANK = 512
LN_EPS = 1e-5
BIT_EPS = 1e-6
Q_B = 128.0
MASKED = -1e30


def transformer_program(nc, x_in, wq_a, wk_a, wv_a, wo_a, w_gate_up, w_down,
                        wq_b, wk_b, wv_b, wo_b, w_fc, w_proj, cos_in, sin_in, out):
    T, C = x_in.shape[1], x_in.shape[2]
    NT = T // P
    KC = C // P
    F = w_down.shape[1]
    NF = F // P
    HEAD = 64
    NG = wk_b.shape[1] // HEAD
    NH = wq_b.shape[1] // HEAD
    assert NH == 4 * NG and T == 1024 and C == 256 and F == 1024

    base = (nc.sbuf_base + 31) // 32 * 32

    def sb(name, kb, shape, dt):
        return nc.alloc_sbuf_tensor_at(name, [P] + shape, dt, offset=base + int(kb * 1024))

    x = sb("x", 0, [NT, C], F32)
    xnT_hi = sb("xnT_hi", 8, [KC, T], F32R)
    xnT_lo = sb("xnT_lo", 16, [KC, T], F32R)
    identf = sb("identf", 24, [P], F32)
    identh = sb("identh", 24.5, [P], F16)
    identb = sb("identb", 24.75, [P], BF16)
    maskb = sb("maskb", 25, [P], BF16)
    stats = sb("stats", 25.25, [6 * NT], F32)
    moments = sb("moments", 25.4375, [4, 2 * NT], F32)
    small = sb("small", 25.6875, [64], F32)
    ones = sb("ones", 207, [P], F32)
    xn = sb("xn", 26, [NT, C], F32)
    wq_a_sb = sb("wq_a_sb", 34, [KC, C], F32)
    wk_a_sb = sb("wk_a_sb", 36, [KC, C], F32)
    wv_a_sb = sb("wv_a_sb", 38, [KC, C], F32)
    wo_a_sb = sb("wo_a_sb", 40, [KC, C], F32)
    wvT_a = sb("wvT_a", 42, [KC, C], F32)
    gram = sb("gram", 44, [KC, C], F32)
    gram_wk = sb("gram_wk", 46, [KC, C], F32)
    attn_a = sb("attn_a", 48, [KC, C], F32)
    attn_wo = sb("attn_wo", 50, [KC, C], F32)
    mix_hi = sb("mix_hi", 52, [KC, C], F32R)
    mix_lo = sb("mix_lo", 54, [KC, C], F32R)
    wdn_nat = sb("wdn_nat", 56, [KC, F], F32)
    wgu_nat = sb("wgu_nat", 64, [2 * NF, C], F32)
    wguT_hi = sb("wguT_hi", 80, [KC, 2 * F], F32R)
    wguT_lo = sb("wguT_lo", 96, [KC, 2 * F], F32R)
    wdnT_hi = sb("wdnT_hi", 112, [NF, C], F32R)
    wdnT_lo = sb("wdnT_lo", 120, [NF, C], F32R)
    silu = sb("silu", 128, [2, BANK], F32)
    h32 = sb("h32", 132, [3, BANK], F32)
    hT_hi = sb("hT_hi", 138, [2 * NF, BANK], F32R)
    hT_lo = sb("hT_lo", 170, [2 * NF, BANK], F32R)
    wfc_nat = sb("wfc_nat", 64, [NF, C], F32)
    wpj_nat = sb("wpj_nat", 72, [KC, F], F32)
    above = sb("above", 202, [2 * F], F16)
    tern = sb("tern", 56, [2, 2 * F], F16)
    fcT = sb("fcT", 96, [KC, F], F16)
    pjT = sb("pjT", 100, [NF, C], F16)
    cosT = sb("cosT", 34, [T], F32)
    sinT = sb("sinT", 38, [T], F32)
    wv_nat = sb("wv_nat", 42, [KC, NG * HEAD], F32)
    wv_hi = sb("wv_hi", 46, [KC, NG * HEAD], F32R)
    wv_lo = sb("wv_lo", 50, [KC, NG * HEAD], F32R)
    v_hi = sb("v_hi", 80, [NT, NG * HEAD], F16)
    v_lo = sb("v_lo", 88, [NT, NG * HEAD], F16)
    wk_nat = sb("wk_nat", 202, [KC, P], F32)
    wq_nat = [sb(f"wq_nat{p}", 203 + p, [KC, P], F32) for p in range(2)]
    wo_nat = sb("wo_nat", 205, [2, C], F32)
    wk_hi = sb("wk_hi", 112, [KC, P], F32R)
    wk_lo = sb("wk_lo", 113, [KC, P], F32R)
    wq_hi = [sb(f"wq_hi{p}", 114 + 2 * p, [KC, P], F32R) for p in range(2)]
    wq_lo = [sb(f"wq_lo{p}", 115 + 2 * p, [KC, P], F32R) for p in range(2)]
    wo_hi = sb("wo_hi", 118, [2, C], F32R)
    wo_lo = sb("wo_lo", 120, [2, C], F32R)
    vg_hi = sb("vg_hi", 122, [NT, HEAD], F16)
    vg_lo = sb("vg_lo", 123, [NT, HEAD], F16)
    k_hh = [sb(f"k_hh{b}", 138 + 8 * b, [T], F32R) for b in range(2)]
    k_ll = [sb(f"k_ll{b}", 142 + 8 * b, [T], F32R) for b in range(2)]
    q_st = [[sb(f"q_st{p}{a}", 154 + 8 * p + 4 * a, [T], F32R) for a in range(2)] for p in range(2)]
    raw = [sb(f"raw{b}", 170 + 4 * b, [T], F32) for b in range(2)]
    swapped = sb("swapped", 178, [T], F32)
    roped = sb("roped", 182, [T], F32)
    pT_hi = [[sb("pT_hi00", 186, [4, BANK], F16), sb("pT_hi01", 26, [8, BANK], F16)],
             [sb("pT_hi10", 190, [4, BANK], F16), sb("pT_hi11", 104, [8, BANK], F16)]]
    pT_lo = [[sb("pT_lo00", 194, [4, BANK], F16), sb("pT_lo01", 128, [8, BANK], F16)],
             [sb("pT_lo10", 198, [4, BANK], F16), sb("pT_lo11", 42, [8, BANK], F16)]]
    recip_b = sb("recip_b", 50, [4, P], F32)
    recipT = sb("recipT", 52, [BANK], F32)
    o32 = sb("o32", 54, [BANK], F32)
    probs = [sb(f"probs{b}", 56 + 4 * b, [T], F32) for b in range(2)]
    oT_hi = sb("oT_hi", 64, [2, T], F32R)
    oT_lo = sb("oT_lo", 72, [2, T], F32R)
    y = sb("y", 26, [NT, C], F32)
    yT_hi = sb("yT_hi", 34, [KC, T], F16)
    yT_lo = sb("yT_lo", 38, [KC, T], F16)
    gelu = sb("gelu", 138, [2, F], F32)
    z = sb("z", 146, [2, F], F32)
    zT_hi = sb("zT_hi", 154, [2, NF, P], F16)
    zT_lo = sb("zT_lo", 158, [2, NF, P], F16)
    zstats = sb("zstats", 162, [NT, 12], F32)
    bit = sb("bit", 163, [12, NT], F32)

    def col(i, n=1):
        return small[:, i:i + n]
    neg_half = col(0)
    abs_sum = col(1, 2)
    gam = col(3, 2)
    thr = col(5, 2)
    nthr = col(7, 2)
    ngam = col(9, 2)
    wv_max = col(11)
    v_inv = col(13)
    v_scale = col(14)
    wv_all = col(15)
    nmax = small[:, 16:20]
    s_nmax = col(20, 2)
    s_scaled = col(22, 2)
    s_sum = col(24, 2)
    s_rec = col(26, 2)
    lsum = small[:, 28:44].rearrange("p (s u) -> p s u", s=2)
    lrec = small[:, 44:60].rearrange("p (s u) -> p s u", s=2)

    def mean_of(st, i):
        return moments[:, st, 2 * i:2 * i + 1]

    with ExitStack() as ctx:
        PS = ctx.enter_context(nc.psum_tensor("PS", [P, 8 * BANK], F32))

        def bank(b, n=1):
            return PS[:, b * BANK:(b + n) * BANK]

        def two_chunks(b):
            return bank(b, 2).rearrange("p (m n) -> p m n", m=2)[:, :, 0:C]

        def sem(name):
            return ctx.enter_context(nc.semaphore(name))

        x_landed = [sem(f"x_landed{j}") for j in range(NT // 2)]
        wa_landed = [sem(f"wa_landed{j}") for j in range(4)]
        wgu_landed = [sem(f"wgu_landed{j}") for j in range(2)]
        wdn_landed = sem("wdn_landed")
        tern_landed = [sem(f"tern_landed{j}") for j in range(2)]
        rope_landed = sem("rope_landed")
        wv_landed = sem("wv_landed")
        wk_landed = sem("wk_landed")
        wq_landed = [sem(f"wq_landed{p}") for p in range(2)]
        wo_landed = sem("wo_landed")
        out_stored = sem("out_stored")
        const_step = sem("const_step")
        const_ready = sem("const_ready")
        stats_done = sem("stats_done")
        moments_done = sem("moments_done")
        var_eps_done = sem("var_eps_done")
        rstd_done = sem("rstd_done")
        xn_done = sem("xn_done")
        xT_done = sem("xT_done")
        xT_hi_done = sem("xT_hi_done")
        xT_lo_done = sem("xT_lo_done")
        x_added = sem("x_added")
        wvT_done, wvT_kept = sem("wvT_done"), sem("wvT_kept")
        chain_pe = sem("chain_pe")
        chain_act = sem("chain_act")
        chain_dve = sem("chain_dve")
        soft_dve = sem("soft_dve")
        soft_act = sem("soft_act")
        mixed_done = sem("mixed_done")
        wT_done, wT_hi_done, wT_lo_done = sem("wT_done"), sem("wT_hi_done"), sem("wT_lo_done")
        gate_up_done, silu_done, h_done = sem("gate_up_done"), sem("silu_done"), sem("h_done")
        h_hi_done, h_lo_done, down_done = sem("h_hi_done"), sem("h_lo_done"), sem("down_done")
        abs_done, gam_sum_done, gam_done = sem("abs_done"), sem("gam_sum_done"), sem("gam_done")
        above_done, tern_done = sem("above_done"), sem("tern_done")
        ternT_done, ternT_kept = sem("ternT_done"), sem("ternT_kept")
        wv_max_done, wv_all_done, v_scale_done = sem("wv_max_done"), sem("wv_all_done"), sem("v_scale_done")
        wv_hi_done, wv_lo_done = sem("wv_hi_done"), sem("wv_lo_done")
        v_done, v_hi_done, v_lo_done = sem("v_done"), sem("v_hi_done"), sem("v_lo_done")
        raw_done, swap_landed, rope_mul = sem("raw_done"), sem("swap_landed"), sem("rope_mul")
        low_q_done = sem("low_q_done")
        roped_done, prod_hi_done, prod_lo_done = sem("roped_done"), sem("prod_hi_done"), sem("prod_lo_done")
        q_landed = [sem(f"q_landed{p}") for p in range(2)]
        wk_split, wo_split = sem("wk_split"), sem("wo_split")
        wq_split = [sem(f"wq_split{p}") for p in range(2)]
        split_hi = sem("split_hi")
        scores_done, nmax_done, exp_done = sem("scores_done"), sem("nmax_done"), sem("exp_done")
        pT_done, pT_hi_done, pT_lo_done = sem("pT_done"), sem("pT_hi_done"), sem("pT_lo_done")
        recip_done, recip_b_done, recipT_done = sem("recip_done"), sem("recip_b_done"), sem("recipT_done")
        vg_done, pv_done = sem("vg_done"), sem("pv_done")
        o_done, o_hi_done, o_lo_done = sem("o_done"), sem("o_hi_done"), sem("o_lo_done")
        misc_done = sem("misc_done")
        bit_step = sem("bit_step")
        y_done = sem("y_done")
        fc_done, gelu_done, z_done = sem("fc_done"), sem("gelu_done"), sem("z_done")
        zT_done, zT_hi_done, zT_lo_done = sem("zT_done"), sem("zT_hi_done"), sem("zT_lo_done")
        z_stats_done, z_moments_done, z_rstd_done = sem("z_stats_done"), sem("z_moments_done"), sem("z_rstd_done")
        z_var_done = sem("z_var_done")
        pj_done, result_done = sem("pj_done"), sem("result_done")

        x_dram = x_in.rearrange("a (i p) c -> p (a i) c", p=P)
        out_dram = out.rearrange("a (i p) c -> p (a i) c", p=P)

        def rows(w):
            return w.rearrange("(c p) n -> p c n", p=P)

        LAG = 2
        UNITS = 32

        def chunks_to(k):
            if k < 0:
                return chunks_to(k + UNITS) - 48
            kk = k % 16
            return 24 * (k // 16) + (kk if kk < 8 else 8 + 2 * (kk - 8))

        def unit(k):
            kk = k % 16
            return (k // 16) % 2, kk // 2, kk % 2

        MISC = {0: "q1_0", 1: "q1_1", 4: "rl3", 5: "k_0", 6: "k_1", 9: "wo_0", 10: "wo_1",
                11: "wo_2", 12: "rl0", 13: "wo_3", 14: "q0_0", 15: "q0_1", 20: "rl1", 28: "rl2"}

        def has(kind, name):
            if kind == "first" and (name == "rl3" or name.startswith("wo")):
                return False
            return not (kind == "last" and name[:2] in ("k_", "q0"))

        def jobs(kind):
            return [n for _, n in sorted(MISC.items()) if has(kind, n)]

        FIRST_JOBS = 4

        def misc_before(g, kind):
            return FIRST_JOBS if kind == "first" else FIRST_JOBS + len(jobs("first")) + (g - 1) * len(jobs("mid"))

        def misc_index(g, kind, name):
            return misc_before(g, kind) + jobs(kind).index(name)

        MISC_TAIL = misc_before(NG - 1, "last") + len(jobs("last"))

        def run_groups(eng, emit):
            emit(0, "first", 0)
            with eng.Fori(0, (NG - 2) // 2) as turn:
                emit(turn * 2 + 1, "mid", 1)
                emit(turn * 2 + 2, "mid", 0)
            emit(NG - 1, "last", (NG - 1) % 2)

        block = ctx.enter_context(nc.Block())

        @block.sync
        def _(sp):
            for j in range(NT // 2):
                sp.dma_start(x[:, 2 * j:2 * j + 2, :], x_dram[:, 2 * j:2 * j + 2, :]).then_inc(x_landed[j], 16)
            for j in range(2):
                sp.dma_start(wgu_nat[:, NF * j:NF * (j + 1), :],
                             rows(w_gate_up)[:, NF * j:NF * (j + 1), :]).then_inc(wgu_landed[j], 16)
            sp.dma_start(wdn_nat[:], rows(w_down)).then_inc(wdn_landed, 16)
            sp.wait_ge(wT_done, 8)
            sp.dma_start(wfc_nat[:], rows(w_fc)).then_inc(tern_landed[0], 16)
            sp.dma_start(wpj_nat[:], rows(w_proj)).then_inc(tern_landed[1], 16)
            sp.wait_ge(mixed_done, 4)
            sp.dma_start(cosT[:], cos_in).then_inc(rope_landed, 16)
            sp.dma_start(sinT[:], sin_in).then_inc(rope_landed, 16)
            sp.dma_start(wv_nat[:], rows(wv_b)).then_inc(wv_landed, 16)

            def load_wk(g):
                for half in range(2):
                    sp.dma_start(wk_nat[:, :, HEAD * half:HEAD * (half + 1)],
                                 rows(wk_b)[:, :, bass.ds(g * HEAD, HEAD)]).then_inc(wk_landed, 16)

            def load_wq(g, p):
                sp.dma_start(wq_nat[p][:], rows(wq_b)[:, :, bass.ds(g * 2 * P + p * P, P)]).then_inc(wq_landed[p], 16)

            def load_wo(g):
                for p in range(2):
                    sp.dma_start(wo_nat[:, p, :], wo_b[bass.ds(g * 2 * P + p * P, P), :]).then_inc(wo_landed, 16)

            sp.wait_ge(tern_done, 2)
            load_wk(0)
            load_wq(0, 0)
            load_wq(0, 1)

            def swap(r, par):
                sp.wait_ge(raw_done, 2 * r + 2)
                if not (isinstance(r, int) and r == 0):
                    sp.wait_ge(roped_done, r)
                for d, s in ((0, 32), (32, 0), (64, 96), (96, 64)):
                    sp.dma_start(swapped[d:d + 32, :], raw[par][s:s + 32, :]).then_inc(swap_landed, 16)

            def spread_lo(r, p, par):
                sp.wait_ge(prod_lo_done, r + 1)
                sp.dma_start(q_st[p][0][64:128, :].bitcast(F32), raw[par][0:64, :]).then_inc(q_landed[p], 16)
                sp.dma_start(q_st[p][1][0:64, :].bitcast(F32), raw[par][64:128, :]).then_inc(q_landed[p], 16)

            swap(0, 0)
            swap(1, 1)
            spread_lo(1, 0, 1)

            def group(g, kind, par):
                if kind != "last":
                    sp.wait_ge(wk_split, g + 1)
                    load_wk(g + 1)
                if kind != "first":
                    sp.wait_ge(misc_done, misc_before(g, kind))
                    load_wo(g - 1)
                if kind != "last":
                    sp.wait_ge(wq_split[0], g + 1)
                    load_wq(g + 1, 0)
                    sp.wait_ge(wq_split[1], g + 1)
                    load_wq(g + 1, 1)
                swap(3 * g + 2, par)
                if kind != "last":
                    swap(3 * g + 3, 1 - par)
                spread_lo(3 * g + 2, 1, par)
                if kind != "last":
                    swap(3 * g + 4, par)
                    spread_lo(3 * g + 4, 0, par)

            run_groups(sp, group)
            sp.wait_ge(wo_split, NG - 1)
            load_wo(NG - 1)
            for t in range(NT):
                sp.wait_ge(result_done, t + 1)
                sp.dma_start(out_dram[:, t, :], x[:, t, :]).then_inc(out_stored, 16)
            sp.wait_ge(out_stored, 16 * NT)

        @block.gpsimd
        def _(pool):
            nc.gpsimd.memset(identf[:], 0.0).then_inc(const_step, 1)
            nc.gpsimd.memset(roped[:, 0:P], 0.0).then_inc(const_step, 1)
            pool.wait_ge(const_step, 2)
            nc.gpsimd.affine_select(out=identf[:], in_=identf[:], compare_op=ALU.not_equal, fill=1.0, base=0,
                                    pattern=[[-1, P]], channel_multiplier=1).then_inc(const_step, 1)
            nc.gpsimd.affine_select(out=roped[:, 0:P], in_=roped[:, 0:P], compare_op=ALU.is_ge, fill=MASKED,
                                    base=0, pattern=[[-1, P]], channel_multiplier=1).then_inc(const_step, 1)
            nc.gpsimd.memset(neg_half, -0.5)
            nc.gpsimd.memset(ones[:], 1.0)
            pool.wait_ge(const_step, 4)
            nc.gpsimd.tensor_copy(identb[:], identf[:])
            nc.gpsimd.tensor_copy(identh[:], identf[:])
            nc.gpsimd.tensor_copy(maskb[:], roped[:, 0:P]).then_inc(const_ready, 1)
            pool.wait_ge(const_ready, 1)

            def rstd(st, i, eps):
                v = moments[:, st, 2 * i + 1:2 * i + 2]
                pool.wait_ge(moments_done, st * NT + i + 1)
                nc.gpsimd.tensor_scalar(v, v, eps, None, ALU.add).then_inc(var_eps_done, 1)
                pool.wait_ge(var_eps_done, st * NT + i + 1)
                nc.gpsimd.tensor_tensor(v, v, neg_half, ALU.pow).then_inc(rstd_done, 1)

            for i in range(NT):
                rstd(0, i, LN_EPS)
            for i in range(NT):
                rstd(1, i, LN_EPS)

            def h_low(n):
                pool.wait_ge(h_hi_done, n + 1)
                nc.gpsimd.tensor_tensor(hT_lo[:, n, :], h32[:, n % 3, :], hT_hi[:, n, :].bitcast(F32),
                                        ALU.subtract).then_inc(h_lo_done, 1)

            for n in range(2 * NF):
                h_low(n)
                if n == 5:
                    pool.wait_ge(wv_max_done, 1)
                    nc.gpsimd.partition_all_reduce(wv_all, wv_max, P, bass.bass_isa.ReduceOp.max)\
                      .then_inc(wv_all_done, 1)
                if n >= 12 and n < 16:
                    rstd(2, n - 12, LN_EPS)

            def split(nat, hi, lo, landed, value, done, count):
                pool.wait_ge(landed, value)
                nc.gpsimd.tensor_copy(hi[:], nat[:]).then_inc(split_hi, 1)
                pool.wait_ge(split_hi, count)
                nc.gpsimd.tensor_tensor(lo[:], nat[:], hi[:].bitcast(F32), ALU.subtract).then_inc(done, 1)

            pool.wait_ge(down_done, 4)
            split(wk_nat, wk_hi, wk_lo, wk_landed, 32, wk_split, 1)
            rstd(2, 4, LN_EPS)
            rstd(2, 5, LN_EPS)
            split(wq_nat[0], wq_hi[0], wq_lo[0], wq_landed[0], 16, wq_split[0], 2)
            rstd(2, 6, LN_EPS)
            rstd(2, 7, LN_EPS)
            split(wq_nat[1], wq_hi[1], wq_lo[1], wq_landed[1], 16, wq_split[1], 3)

            def rope(r, par):
                if not (isinstance(r, int) and r == 0):
                    pool.wait_ge(prod_lo_done, r)
                pool.wait_ge(raw_done, 2 * r + 2)
                nc.gpsimd.tensor_tensor(roped[:], raw[par][:], cosT[:], ALU.mult).then_inc(rope_mul, 1)
                pool.wait_ge(swap_landed, r * 64 + 64)
                nc.gpsimd.tensor_tensor(swapped[:], swapped[:], sinT[:], ALU.mult).then_inc(rope_mul, 1)
                pool.wait_ge(rope_mul, 2 * r + 2)
                nc.gpsimd.tensor_tensor(roped[:], roped[:], swapped[:], ALU.add).then_inc(roped_done, 1)

            def low_q(r, p, par, count):
                pool.wait_ge(prod_hi_done, r + 1)
                nc.gpsimd.tensor_tensor(raw[par][0:64, :], roped[0:64, :], q_st[p][0][0:64, :].bitcast(F32),
                                        ALU.subtract).then_inc(low_q_done, 1)
                pool.wait_ge(low_q_done, count)
                nc.gpsimd.tensor_tensor(raw[par][64:128, :], roped[64:128, :], q_st[p][1][64:128, :].bitcast(F32),
                                        ALU.subtract).then_inc(prod_lo_done, 1)
                pool.wait_ge(prod_lo_done, r + 1)

            def low_k(r, slot):
                pool.wait_ge(prod_hi_done, r + 1)
                nc.gpsimd.tensor_tensor(k_ll[slot][:], roped[:], k_hh[slot][:].bitcast(F32),
                                        ALU.subtract).then_inc(prod_lo_done, 1)

            def low_o(s, m):
                p, half = m // 2, m % 2
                pool.wait_ge(o_hi_done, s + 1)
                nc.gpsimd.tensor_tensor(oT_lo[:, p, half * BANK:(half + 1) * BANK], o32[:],
                                        oT_hi[:, p, half * BANK:(half + 1) * BANK].bitcast(F32),
                                        ALU.subtract).then_inc(o_lo_done, 1)

            pool.wait_ge(rope_landed, 32)
            rope(0, 0)
            low_k(0, 0)
            rope(1, 1)
            low_q(1, 0, 1, 1)

            def group(g, kind, par):
                rope(3 * g + 2, par)
                if kind != "first":
                    low_o(4 * g - 1, 3)
                low_q(3 * g + 2, 1, par, 2 * g + 2)
                if kind != "last":
                    rope(3 * g + 3, 1 - par)
                low_o(4 * g, 0)
                if kind != "last":
                    low_k(3 * g + 3, 1 - par)
                    rope(3 * g + 4, par)
                low_o(4 * g + 1, 1)
                if kind != "last":
                    low_q(3 * g + 4, 0, par, 2 * g + 3)
                low_o(4 * g + 2, 2)

            run_groups(pool, group)
            low_o(4 * NG - 1, 3)
            for i in range(NT):
                rstd(3, i, BIT_EPS)
            for t in range(NT):
                v = zstats[:, t, 1:2]
                pool.wait_ge(z_moments_done, t + 1)
                nc.gpsimd.tensor_scalar(v, v, BIT_EPS, None, ALU.add).then_inc(z_var_done, 1)
                pool.wait_ge(z_var_done, t + 1)
                nc.gpsimd.tensor_tensor(v, v, neg_half, ALU.pow).then_inc(z_rstd_done, 1)

        @block.scalar
        def _(act):
            for j, (w, dst) in enumerate(((wk_a, wk_a_sb), (wq_a, wq_a_sb), (wv_a, wv_a_sb), (wo_a, wo_a_sb))):
                act.dma_start(dst[:], rows(w)).then_inc(wa_landed[j], 16)

            def x_high(st, hf, c, b):
                act.wait_ge(xT_done, 4 * st + 2 * hf + c + 1)
                dst = (yT_hi if st == 3 else xnT_hi)[:, c, hf * BANK:(hf + 1) * BANK]
                nc.scalar.copy(dst, bank(b)).then_inc(xT_hi_done, 1)

            act.wait_ge(wvT_done, 1)
            nc.scalar.copy(wvT_a[:], bank(2).rearrange("p (c n) -> p c n", c=KC)).then_inc(wvT_kept, 1)
            for hf in range(2):
                for c in range(KC):
                    x_high(0, hf, c, 4 + 2 * hf + c)

            def w_high(k):
                act.wait_ge(wT_done, k + 1)
                dst = wguT_hi[:, k % 2, (k // 2) * BANK:(k // 2 + 1) * BANK] if k < 8 else wdnT_hi[:, 2 * (k - 8):2 * (k - 7), :]
                src = bank(4 + k % 4) if k < 8 else bank(4 + k % 4).rearrange("p (i n) -> p i n", i=2)
                nc.scalar.copy(dst, src).then_inc(wT_hi_done, 1)

            act.wait_ge(chain_pe, 1)
            nc.scalar.copy(gram[:, 0, :], bank(0)[:, 0:C]).then_inc(chain_act, 1)
            act.wait_ge(chain_pe, 3)
            nc.scalar.copy(gram_wk[:, 0, :], bank(2)[:, 0:C]).then_inc(chain_act, 1)
            w_high(0)
            w_high(1)
            for m in range(KC):
                act.wait_ge(soft_dve, 2)
                nc.scalar.activation(attn_a[:, m, :], bank(m)[:, 0:C], ACT.Exp,
                                     bias=s_scaled[:, m:m + 1], scale=8 ** -0.5,
                                     accum_out=s_sum[:, m:m + 1]).then_inc(soft_act, 1)
            for k in range(2, 6):
                w_high(k)
            act.wait_ge(chain_pe, 7)
            nc.scalar.copy(attn_wo[:, 0, :], bank(2)[:, 0:C]).then_inc(chain_act, 1)
            w_high(6)
            w_high(7)
            act.wait_ge(chain_pe, 10)
            nc.scalar.copy(mix_hi[:], two_chunks(0)).then_inc(chain_act, 1)
            for k in range(8, 12):
                w_high(k)

            for hf in range(2):
                for c in range(KC):
                    x_high(1, hf, c, 4 + 2 * hf + c)
            for n in range(2 * NF):
                act.wait_ge(gate_up_done, n + 1)
                if n >= 2:
                    act.wait_ge(h_done, n - 1)
                nc.scalar.activation(silu[:, n % 2, :], bank(2 * (n % 2)), ACT.Silu).then_inc(silu_done, 1)
                if n in (5, 7):
                    m = (n - 5) // 2
                    act.wait_ge(tern_landed[m], 16)
                    if m:
                        act.wait_ge(abs_done, 1)
                    nat = (wfc_nat, wpj_nat)[m]
                    nc.scalar.activation(above[:].rearrange("p (a b) -> p a b", a=nat.shape[1]), nat[:], ACT.Abs,
                                         accum_out=abs_sum[:, m:m + 1]).then_inc(abs_done, 1)
                if n == 9:
                    act.wait_ge(wv_landed, 16)
                    nc.scalar.copy(wv_hi[:], wv_nat[:]).then_inc(wv_hi_done, 1)

            def raw_half(r, par, half, job, scale, guard=None):
                act.wait_ge(misc_done, job + 1)
                if half == 0 and guard is not None:
                    guard()
                nc.scalar.mul(raw[par][:, half * BANK:(half + 1) * BANK], bank(7), scale).then_inc(raw_done, 1)

            Q_SCALE = HEAD ** -0.5

            def high_q(r, p):
                act.wait_ge(roped_done, r + 1)
                nc.scalar.copy(q_st[p][0][0:64, :], roped[0:64, :])
                nc.scalar.copy(q_st[p][1][64:128, :], roped[64:128, :]).then_inc(prod_hi_done, 1)

            def high_k(r, slot):
                act.wait_ge(roped_done, r + 1)
                nc.scalar.copy(k_hh[slot][:], roped[:]).then_inc(prod_hi_done, 1)

            for hf in range(2):
                for c in range(KC):
                    x_high(2, hf, c, 2 * hf + c)
            raw_half(0, 0, 0, 0, 1.0)
            raw_half(0, 0, 1, 1, 1.0)
            raw_half(1, 1, 0, 2, Q_SCALE)
            raw_half(1, 1, 1, 3, Q_SCALE)
            for t in range(NT):
                act.wait_ge(v_done, t + 1)
                act.wait_ge(v_scale_done, 3)
                nc.scalar.activation(v_hi[:, t, :], bank(4 + t % 3), ACT.Copy, scale=v_scale).then_inc(v_hi_done, 1)
            high_k(0, 0)
            high_q(1, 0)

            def exp_unit(g, kind, k):
                p, i, a = unit(k)
                n = 32 * g + k
                width = (i + 1) * P
                act.wait_ge(nmax_done, n + 1)
                if not (kind == "first" and k < 2):
                    act.wait_ge(pT_done, 48 * g + chunks_to(k - 1))
                m = 2 * p + i // 4
                nc.scalar.activation(probs[k % 2][:, 0:width], PS[:, (k % 2) * 2 * BANK:(k % 2) * 2 * BANK + width],
                                     ACT.Exp, bias=nmax[:, k % 4:k % 4 + 1],
                                     accum_out=lsum[:, m % 2, (i % 4) * 2 + a:(i % 4) * 2 + a + 1])\
                  .then_inc(exp_done, 1)

            def evacuate_hi(g, kind, k):
                p, i, a = unit(k)
                half = i // 4
                s = 4 * g + (2 * p + half if k >= 0 else -1)
                for c in range(i // 4 + 1):
                    q = chunks_to(k) + c
                    j0, j1 = 4 * c, min(4 * c + 4, i + 1)
                    act.wait_ge(pT_done, 48 * g + q + 1)
                    if c == 0 and k % 8 < 2 and not (kind == "first" and 0 <= k < 16):
                        act.wait_ge(pv_done, s - 1)
                    dst = pT_hi[a][half][:, j0:j1, (i % 4) * P:(i % 4 + 1) * P]
                    nc.scalar.copy(dst, bank(4 + q % 2)[:, 0:(j1 - j0) * P].rearrange("p (j n) -> p j n", n=P))\
                      .then_inc(pT_hi_done, 1)

            def recip_out(g, kind, m, job):
                s = 4 * g + m
                act.wait_ge(misc_done, job + 1)
                if not (kind == "first" and m == 0):
                    act.wait_ge(o_done, s)
                nc.scalar.copy(recipT[:], bank(7)).then_inc(recipT_done, 1)

            def high_o(g, kind, m):
                s, mm = 4 * g + m, m % 4
                p, half = mm // 2, mm % 2
                act.wait_ge(o_done, s + 1)
                if m == 0 and kind != "first":
                    act.wait_ge(misc_done, misc_index(g, kind, "wo_3") + 1)
                nc.scalar.copy(oT_hi[:, p, half * BANK:(half + 1) * BANK], o32[:]).then_inc(o_hi_done, 1)

            def group(g, kind, par):
                for k in range(UNITS):
                    job = MISC.get(k - 1)
                    if job and has(kind, job):
                        index, last_char = misc_index(g, kind, job), int(job[-1])
                        if job[:2] == "q1":
                            raw_half(3 * g + 2, par, last_char, index, Q_SCALE,
                                     lambda: act.wait_ge(roped_done, 3 * g + 1))
                        elif job[:2] == "k_":
                            raw_half(3 * g + 3, 1 - par, last_char, index, 1.0,
                                     lambda: act.wait_ge(q_landed[0], 32 * g + 32))
                        elif job[:2] == "q0":
                            raw_half(3 * g + 4, par, last_char, index, Q_SCALE,
                                     lambda: act.wait_ge(q_landed[1], 32 * g + 32))
                        elif job[:2] == "rl":
                            recip_out(g, kind, -1 if last_char == 3 else last_char, index)
                    if not (kind == "first" and k < LAG):
                        evacuate_hi(g, kind, k - LAG)
                    exp_unit(g, kind, k)
                    if k % 8 == 7 and not (kind == "first" and k == 7):
                        high_o(g, kind, k // 8 - 1)
                    if k == 9:
                        high_q(3 * g + 2, 1)
                    if k == 16 and kind != "last":
                        high_k(3 * g + 3, 1 - par)
                    if k == 22 and kind != "last":
                        high_q(3 * g + 4, 0)

            run_groups(act, group)
            g = NG
            evacuate_hi(g, "mid", -2)
            evacuate_hi(g, "mid", -1)
            recip_out(g, "mid", -1, MISC_TAIL)
            high_o(g, "mid", -1)

            for hf in range(2):
                for c in range(KC):
                    x_high(3, hf, c, 2 * hf + c)

            def z_high(t):
                act.wait_ge(zT_done, t + 1)
                nc.scalar.copy(zT_hi[:, t % 2], bank(4, 2).rearrange("p (i n) -> p i n", i=NF)).then_inc(zT_hi_done, 1)

            for t in range(NT):
                act.wait_ge(fc_done, t + 1)
                if t >= 2:
                    act.wait_ge(z_done, 2 * t - 3)
                nc.scalar.activation(gelu[:, t % 2, :], bank(2 * (t % 2), 2), ACT.Gelu,
                                     scale=bit[:, 3, t:t + 1]).then_inc(gelu_done, 1)
                if t >= 1:
                    z_high(t - 1)
            z_high(NT - 1)

        @block.vector
        def _(dve):
            def tile_moments(st, i):
                nc.vector.bn_stats(stats[:, 6 * i:6 * i + 6], x[:, i, :]).then_inc(stats_done, 1)
                dve.wait_ge(stats_done, st * NT + i + 1)
                nc.vector.bn_aggr(moments[:, st, 2 * i:2 * i + 2], stats[:, 6 * i:6 * i + 6]).then_inc(moments_done, 1)

            def normalise(st, i):
                dve.wait_ge(rstd_done, st * NT + i + 1)
                nc.vector.tensor_scalar(xn[:, i, :], x[:, i, :], mean_of(st, i), moments[:, st, 2 * i + 1:2 * i + 2],
                                        ALU.subtract, ALU.mult).then_inc(xn_done, 1)

            def x_low(st, hf, c, b):
                dve.wait_ge(xT_hi_done, 4 * st + 2 * hf + c + 1)
                sl = slice(hf * BANK, (hf + 1) * BANK)
                nc.vector.tensor_tensor(xnT_lo[:, c, sl], bank(b), xnT_hi[:, c, sl].bitcast(F32),
                                        ALU.subtract).then_inc(xT_lo_done, 1)

            for i in range(NT):
                dve.wait_ge(x_landed[i // 2], 16)
                tile_moments(0, i)
                if i:
                    normalise(0, i - 1)
            normalise(0, NT - 1)
            for hf in range(2):
                for c in range(KC):
                    x_low(0, hf, c, 4 + 2 * hf + c)

            def w_low(k):
                dve.wait_ge(wT_hi_done, k + 1)
                if k < 8:
                    sl = slice((k // 2) * BANK, (k // 2 + 1) * BANK)
                    nc.vector.tensor_tensor(wguT_lo[:, k % 2, sl], bank(4 + k % 4), wguT_hi[:, k % 2, sl].bitcast(F32),
                                            ALU.subtract).then_inc(wT_lo_done, 1)
                else:
                    sl = slice(2 * (k - 8), 2 * (k - 7))
                    nc.vector.tensor_tensor(wdnT_lo[:, sl, :], bank(4 + k % 4).rearrange("p (i n) -> p i n", i=2),
                                            wdnT_hi[:, sl, :].bitcast(F32), ALU.subtract).then_inc(wT_lo_done, 1)

            dve.wait_ge(chain_pe, 2)
            nc.vector.tensor_copy(gram[:, 1, :], bank(1)[:, 0:C]).then_inc(chain_dve, 1)
            dve.wait_ge(chain_pe, 4)
            nc.vector.tensor_copy(gram_wk[:, 1, :], bank(3)[:, 0:C]).then_inc(chain_dve, 1)
            w_low(0)
            w_low(1)
            dve.wait_ge(chain_pe, 6)
            nc.vector.tensor_reduce(s_nmax, two_chunks(0), AX.X, ALU.max,
                                    negate=True).then_inc(soft_dve, 1)
            dve.wait_ge(soft_dve, 1)
            nc.vector.tensor_scalar(s_scaled, s_nmax, 8 ** -0.5, None, ALU.mult).then_inc(soft_dve, 1)
            dve.wait_ge(soft_act, 2)
            nc.vector.reciprocal(s_rec, s_sum).then_inc(soft_dve, 1)
            dve.wait_ge(soft_dve, 3)
            for m in range(KC):
                nc.vector.tensor_scalar(attn_a[:, m, :], attn_a[:, m, :], s_rec[:, m:m + 1], None,
                                        ALU.mult).then_inc(soft_dve, 1)
            for k in range(2, 6):
                w_low(k)
            dve.wait_ge(chain_pe, 8)
            nc.vector.tensor_copy(attn_wo[:, 1, :], bank(3)[:, 0:C]).then_inc(chain_dve, 1)
            w_low(6)
            w_low(7)
            dve.wait_ge(chain_act, 4)
            nc.vector.tensor_tensor(mix_lo[:], two_chunks(0), mix_hi[:].bitcast(F32),
                                    ALU.subtract).then_inc(chain_dve, 1)
            for k in range(8, 12):
                w_low(k)

            def add_pair(j, b, count):
                nc.vector.tensor_tensor(x[:, 2 * j:2 * j + 2, :], bank(b).rearrange("p (t n) -> p t n", t=2),
                                        x[:, 2 * j:2 * j + 2, :], ALU.add).then_inc(x_added, 1)
                dve.wait_ge(x_added, count)

            for j in range(4):
                dve.wait_ge(mixed_done, j + 1)
                add_pair(j, j, j + 1)
                for i in (2 * j, 2 * j + 1):
                    tile_moments(1, i)
                    if i:
                        normalise(1, i - 1)
            normalise(1, NT - 1)
            for hf in range(2):
                for c in range(KC):
                    x_low(1, hf, c, 4 + 2 * hf + c)

            def h_tile(n):
                dve.wait_ge(silu_done, n + 1)
                if n >= 3:
                    dve.wait_ge(h_lo_done, n - 2)
                nc.vector.tensor_tensor(h32[:, n % 3, :], silu[:, n % 2, :], bank(2 * (n % 2) + 1),
                                        ALU.mult).then_inc(h_done, 1)
                dve.wait_ge(h_done, n + 1)
                nc.vector.tensor_copy(hT_hi[:, n, :], h32[:, n % 3, :]).then_inc(h_hi_done, 1)

            def add_down(j):
                dve.wait_ge(down_done, j + 1)
                add_pair(j, 4 + j, 4 + j + 1)

            def ternary(m):
                nat = ((wfc_nat, wpj_nat)[m])[:].rearrange("p a b -> p (a b)")
                if m:
                    dve.wait_ge(tern_done, 1)
                nc.vector.tensor_scalar(above[:], nat, thr[:, m:m + 1], None, ALU.is_gt).then_inc(above_done, 1)
                dve.wait_ge(above_done, m + 1)
                nc.vector.scalar_tensor_tensor(out=tern[:, m, :], in0=nat, scalar=nthr[:, m:m + 1], in1=above[:],
                                               op0=ALU.is_lt, op1=ALU.subtract).then_inc(tern_done, 1)

            for n in range(2 * NF):
                h_tile(n)
                if n == 3:
                    dve.wait_ge(wv_landed, 16)
                    nc.vector.tensor_reduce(wv_max, wv_nat[:].rearrange("p c n -> p (c n)"), AX.X, ALU.max,
                                            apply_absolute_value=True).then_inc(wv_max_done, 1)
                if n == 8:
                    dve.wait_ge(wv_all_done, 1)
                    nc.vector.tensor_scalar(wv_max, wv_all, 1e-30, None, ALU.max).then_inc(v_scale_done, 1)
                    dve.wait_ge(v_scale_done, 1)
                    nc.vector.tensor_scalar(v_inv, wv_max, 1.0 / 128, None, ALU.mult).then_inc(v_scale_done, 1)
                    dve.wait_ge(v_scale_done, 2)
                    nc.vector.reciprocal(v_scale, v_inv).then_inc(v_scale_done, 1)
                    dve.wait_ge(gam_sum_done, 1)
                    nc.vector.tensor_scalar(gam, bank(4)[:, 0:2], 1.0 / (F * C), None, ALU.mult).then_inc(gam_done, 1)
                    dve.wait_ge(gam_done, 1)
                    nc.vector.tensor_scalar(thr, gam, BIT_EPS, 0.5, ALU.add, ALU.mult).then_inc(gam_done, 1)
                    nc.vector.tensor_scalar(ngam, gam, -1.0, None, ALU.mult).then_inc(gam_done, 1)
                    dve.wait_ge(gam_done, 3)
                    nc.vector.tensor_scalar(nthr, thr, -1.0, None, ALU.mult).then_inc(gam_done, 1)
                    dve.wait_ge(gam_done, 4)
                if n == 9:
                    ternary(0)
                if n == 10:
                    dve.wait_ge(wv_hi_done, 1)
                    nc.vector.tensor_tensor(wv_lo[:], wv_nat[:], wv_hi[:].bitcast(F32),
                                            ALU.subtract).then_inc(wv_lo_done, 1)
                if n == 11:
                    ternary(1)
                    add_down(0)
                    tile_moments(2, 0)
                    tile_moments(2, 1)
                if n == 13:
                    add_down(1)
                    tile_moments(2, 2)
                    tile_moments(2, 3)
                    normalise(2, 0)
                if n == 15:
                    normalise(2, 1)
                    normalise(2, 2)
                    normalise(2, 3)

            for j in (2, 3):
                add_down(j)
                for i in (2 * j, 2 * j + 1):
                    tile_moments(2, i)
                if j == 2:
                    x_low(2, 0, 0, 0)
                    x_low(2, 0, 1, 1)
            for i in range(4, NT):
                normalise(2, i)
            for c in range(KC):
                x_low(2, 1, c, 2 + c)

            for t in range(NT):
                dve.wait_ge(v_hi_done, t + 1)
                nc.vector.scalar_tensor_tensor(out=v_lo[:, t, :], in0=bank(4 + t % 3), scalar=v_scale, in1=v_hi[:, t, :],
                                               op0=ALU.mult, op1=ALU.subtract).then_inc(v_lo_done, 1)
            for q in range(4):
                dve.wait_ge(ternT_done, q + 1)
                src = bank(q).bitcast(F16)
                if q < 2:
                    nc.vector.tensor_copy(fcT[:, q, :], src).then_inc(ternT_kept, 1)
                else:
                    nc.vector.tensor_copy(pjT[:, 4 * (q - 2):4 * (q - 1), :],
                                          src.rearrange("p (i n) -> p i n", i=4)).then_inc(ternT_kept, 1)

            def row_max(g, kind, k):
                p, i, a = unit(k)
                dve.wait_ge(scores_done, 32 * g + k + 1)
                nc.vector.tensor_reduce(nmax[:, k % 4:k % 4 + 1],
                                        PS[:, (k % 2) * 2 * BANK:(k % 2) * 2 * BANK + (i + 1) * P], AX.X, ALU.max,
                                        negate=True).then_inc(nmax_done, 1)

            def evacuate_lo(g, k):
                p, i, a = unit(k)
                half = i // 4
                for c in range(i // 4 + 1):
                    q = chunks_to(k) + c
                    j0, j1 = 4 * c, min(4 * c + 4, i + 1)
                    sl = (slice(None), slice(j0, j1), slice((i % 4) * P, (i % 4 + 1) * P))
                    dve.wait_ge(pT_hi_done, 48 * g + q + 1)
                    nc.vector.tensor_tensor(pT_lo[a][half][sl],
                                            bank(4 + q % 2)[:, 0:(j1 - j0) * P].rearrange("p (j n) -> p j n", n=P),
                                            pT_hi[a][half][sl], ALU.subtract).then_inc(pT_lo_done, 1)

            def recips(g, kind, m, used=None):
                s, b = 4 * g + m, m % 2
                if m == -1:
                    dve.wait_ge(exp_done, 32 * g)
                else:
                    dve.wait_ge(exp_done, 32 * g + 8 * m + 8)
                nc.vector.reciprocal(lrec[:, b, :], lsum[:, b, :]).then_inc(recip_done, 1)
                dve.wait_ge(recip_done, s + 1)
                if m == -1:
                    dve.wait_ge(misc_done, misc_before(g, kind) if used is None else used)
                elif m > 0:
                    dve.wait_ge(misc_done, misc_index(g, kind, f"rl{m - 1}") + 1)
                elif kind != "first":
                    dve.wait_ge(misc_done, misc_index(g, kind, "rl3") + 1)
                nc.vector.tensor_scalar(recip_b[:].rearrange("p i (a d) -> p (i a) d", a=2),
                                        lrec[:, b, :].unsqueeze(2).broadcast_to([P, 8, HEAD]), v_inv, None,
                                        ALU.mult).then_inc(recip_b_done, 1)

            def scale_o(g, kind, m):
                s = 4 * g + m
                dve.wait_ge(pv_done, s + 1)
                dve.wait_ge(recipT_done, s + 1)
                if not (kind == "first" and m == 0):
                    dve.wait_ge(o_lo_done, s)
                nc.vector.tensor_tensor(o32[:], bank(6), recipT[:], ALU.mult).then_inc(o_done, 1)

            def split(nat, hi, lo, landed, value, used, done, count):
                dve.wait_ge(landed, value)
                dve.wait_ge(misc_done, used)
                nc.vector.tensor_copy(hi[:], nat[:]).then_inc(split_hi, 1)
                dve.wait_ge(split_hi, count)
                nc.vector.tensor_tensor(lo[:], nat[:], hi[:].bitcast(F32), ALU.subtract).then_inc(done, 1)

            def splits_before(g, kind):
                return 3 if kind == "first" else 3 + 3 + 4 * (g - 1)

            def group(g, kind, par):
                n_split = splits_before(g, kind)
                at = [0]

                def next_split():
                    at[0] += 1
                    return n_split + at[0]

                for k in range(UNITS):
                    if k % 8 == 7 and not (kind == "first" and k == 7):
                        scale_o(g, kind, k // 8 - 1)
                    job = MISC.get(k - 1)
                    if job and has(kind, job) and job[:2] == "wo":
                        j = int(job[-1])
                        dve.wait_ge(misc_done, misc_index(g, kind, job) + 1)
                        nc.vector.tensor_tensor(x[:, 2 * j:2 * j + 2, :], bank(7).rearrange("p (t n) -> p t n", t=2),
                                                x[:, 2 * j:2 * j + 2, :], ALU.add).then_inc(x_added, 1)
                    row_max(g, kind, k)
                    if not (kind == "first" and k < LAG):
                        evacuate_lo(g, k - LAG)
                    if k % 8 == 0 and not (kind == "first" and k == 0):
                        recips(g, kind, k // 8 - 1)
                    if k == 3 and kind != "last":
                        split(wk_nat, wk_hi, wk_lo, wk_landed, 32 * g + 64, misc_before(g, kind), wk_split, next_split())
                    if k == 7:
                        if kind != "first":
                            dve.wait_ge(pv_done, 4 * g)
                        nc.vector.tensor_copy(vg_hi[:], v_hi[:, :, bass.ds(g * HEAD, HEAD)])
                        nc.vector.tensor_copy(vg_lo[:], v_lo[:, :, bass.ds(g * HEAD, HEAD)]).then_inc(vg_done, 1)
                    if k == 7 and kind != "first":
                        split(wo_nat, wo_hi, wo_lo, wo_landed, 32 * g, misc_before(g, kind), wo_split, next_split())
                    if k == 12 and kind != "last":
                        split(wq_nat[0], wq_hi[0], wq_lo[0], wq_landed[0], 16 * g + 32, misc_before(g, kind),
                              wq_split[0], next_split())
                    if k == 24 and kind != "last":
                        split(wq_nat[1], wq_hi[1], wq_lo[1], wq_landed[1], 16 * g + 32,
                              misc_index(g, kind, "q1_1") + 1, wq_split[1], next_split())

            run_groups(dve, group)
            g = NG
            evacuate_lo(g, -2)
            evacuate_lo(g, -1)
            recips(g, "mid", -1, MISC_TAIL)
            split(wo_nat, wo_hi, wo_lo, wo_landed, 32 * NG, MISC_TAIL, wo_split,
                  splits_before(NG - 1, "last") + 2)
            scale_o(g, "mid", -1)
            ADDS = 8 + 4 * (NG - 1)
            for j in range(4):
                dve.wait_ge(misc_done, MISC_TAIL + 2 + j)
                dve.wait_ge(x_added, ADDS + j)
                nc.vector.tensor_tensor(x[:, 2 * j:2 * j + 2, :], bank(7).rearrange("p (t n) -> p t n", t=2),
                                        x[:, 2 * j:2 * j + 2, :], ALU.add).then_inc(x_added, 1)
                dve.wait_ge(x_added, ADDS + j + 1)
                for i in (2 * j, 2 * j + 1):
                    tile_moments(3, i)

            steps = [0]

            def step(ins):
                steps[0] += 1
                ins.then_inc(bit_step, 1)
                dve.wait_ge(bit_step, steps[0])

            def quant_scales(am, rstd, ng, g128, s, o):
                step(nc.vector.tensor_tensor(g128, am, rstd, ALU.mult))
                step(nc.vector.tensor_scalar(g128, g128, 1.0 / Q_B, None, ALU.mult))
                step(nc.vector.reciprocal(s, g128))
                step(nc.vector.tensor_tensor(s, s, rstd, ALU.mult))
                step(nc.vector.tensor_scalar(o, g128, ng, None, ALU.mult))

            rstds = moments[:, 3, :].rearrange("p (i two) -> p i two", two=2)
            for hf in range(2):
                tiles = slice(4 * hf, 4 * hf + 4)
                for i in range(4 * hf, 4 * hf + 4):
                    step(nc.vector.tensor_scalar(y[:, i, :], x[:, i, :], mean_of(3, i), None, ALU.subtract))
                step(nc.vector.tensor_reduce(bit[:, 0, tiles], y[:, tiles, :], AX.X, ALU.max, apply_absolute_value=True))
                dve.wait_ge(rstd_done, 3 * NT + 4 * hf + 4)
                quant_scales(bit[:, 0, tiles], rstds[:, tiles, 1], ngam[:, 0:1], bit[:, 1, tiles], bit[:, 2, tiles],
                             bit[:, 3, tiles])
                for i in range(4 * hf, 4 * hf + 4):
                    nc.vector.tensor_scalar(y[:, i, :], y[:, i, :], bit[:, 2, i:i + 1], Q_B, ALU.mult,
                                            ALU.min).then_inc(y_done, 1)
            for hf in range(2):
                for c in range(KC):
                    dve.wait_ge(xT_hi_done, 12 + 2 * hf + c + 1)
                    sl = slice(hf * BANK, (hf + 1) * BANK)
                    nc.vector.scalar_tensor_tensor(out=yT_lo[:, c, sl], in0=bank(2 * hf + c), scalar=-Q_B,
                                                   in1=yT_hi[:, c, sl], op0=ALU.max,
                                                   op1=ALU.subtract).then_inc(xT_lo_done, 1)

            def finish(t):
                dve.wait_ge(zT_hi_done, t + 1)
                nc.vector.scalar_tensor_tensor(out=zT_lo[:, t % 2], in0=bank(4, 2).rearrange("p (i n) -> p i n", i=NF),
                                               scalar=-Q_B, in1=zT_hi[:, t % 2], op0=ALU.max,
                                               op1=ALU.subtract).then_inc(zT_lo_done, 1)

            def result(t):
                dve.wait_ge(pj_done, t + 1)
                nc.vector.scalar_tensor_tensor(out=x[:, t, :], in0=bank(6 + t % 2)[:, 0:C], scalar=bit[:, 7, t:t + 1],
                                               in1=x[:, t, :], op0=ALU.mult, op1=ALU.add).then_inc(result_done, 1)

            for t in range(NT):
                dve.wait_ge(gelu_done, t + 1)
                raw_st = bit[:, 8:12, :].rearrange("p a b -> p (a b)")[:, 0:12]
                for c in range(2):
                    last = nc.vector.bn_stats(raw_st[:, 6 * c:6 * c + 6], gelu[:, t % 2, c * BANK:(c + 1) * BANK])
                step(last)
                nc.vector.bn_aggr(zstats[:, t, 0:2], raw_st).then_inc(z_moments_done, 1)
                dve.wait_ge(z_moments_done, t + 1)
                if t >= 2:
                    dve.wait_ge(zT_done, t - 1)
                nc.vector.tensor_scalar(z[:, t % 2, :], gelu[:, t % 2, :], zstats[:, t, 0:1], None,
                                        ALU.subtract).then_inc(z_done, 1)
                dve.wait_ge(z_done, 2 * t + 1)
                step(nc.vector.tensor_reduce(bit[:, 4, t:t + 1], z[:, t % 2, :], AX.X, ALU.max,
                                             apply_absolute_value=True))
                dve.wait_ge(z_rstd_done, t + 1)
                quant_scales(bit[:, 4, t:t + 1], zstats[:, t, 1:2], ngam[:, 1:2], bit[:, 5, t:t + 1],
                             bit[:, 6, t:t + 1], bit[:, 7, t:t + 1])
                nc.vector.tensor_scalar(z[:, t % 2, :], z[:, t % 2, :], bit[:, 6, t:t + 1], Q_B, ALU.mult,
                                        ALU.min).then_inc(z_done, 1)
                if t >= 1:
                    finish(t - 1)
                if t >= 2:
                    result(t - 2)
            finish(NT - 1)
            result(NT - 2)
            result(NT - 1)

        @block.tensor
        def _(pe):
            def product(dst, pairs):
                for n, (lhsT, rhs) in enumerate(pairs):
                    last = nc.tensor.matmul(dst, lhsT, rhs, start=n == 0, stop=n == len(pairs) - 1)
                return last

            def three(lhs, rhs):
                return [(lhs[0], rhs[0]), (lhs[1], rhs[0]), (lhs[0], rhs[1])]

            def x_transposes(st, hf, first_bank):
                src = y if st == 3 else xn
                for c in range(KC):
                    for q in range(4):
                        i = 4 * hf + q
                        if c == 0:
                            pe.wait_ge(y_done if st == 3 else xn_done, (0 if st == 3 else st * NT) + i + 1)
                        last = nc.tensor.transpose(bank(first_bank + 2 * hf + c)[:, q * P:(q + 1) * P],
                                                   src[:, i, c * P:(c + 1) * P], identf[:])
                    last.then_inc(xT_done, 1)

            pe.wait_ge(const_ready, 1)
            pe.wait_ge(wa_landed[2], 16)
            for f in range(KC):
                for c in range(KC):
                    last = nc.tensor.transpose(bank(2)[:, f * C + c * P:f * C + (c + 1) * P],
                                               wv_a_sb[:, c, f * P:(f + 1) * P], identf[:])
            last.then_inc(wvT_done, 1)
            for hf in range(2):
                x_transposes(0, hf, 4)
            for m in range(KC):
                product(bank(m)[:, 0:C], [(xn[:, i, m * P:(m + 1) * P], xn[:, i, :]) for i in range(NT)])\
                    .then_inc(chain_pe, 1)

            def w_transposes(k):
                if k == 0:
                    pe.wait_ge(wgu_landed[0], 16)
                if k == 4:
                    pe.wait_ge(wgu_landed[1], 16)
                if k == 8:
                    pe.wait_ge(wdn_landed, 16)
                if k < 4:
                    pe.wait_ge(xT_lo_done, k + 1)
                else:
                    pe.wait_ge(wT_lo_done, k - 3)
                for q in range(4):
                    src = wgu_nat[:, 4 * (k // 2) + q, (k % 2) * P:(k % 2 + 1) * P] if k < 8 else \
                        wdn_nat[:, q % 2, (2 * (k - 8) + q // 2) * P:(2 * (k - 8) + q // 2 + 1) * P]
                    last = nc.tensor.transpose(bank(4 + k % 4)[:, q * P:(q + 1) * P], src, identf[:])
                last.then_inc(wT_done, 1)

            def chain(dst_bank, lhs, rhs):
                for m in range(KC):
                    product(bank(dst_bank + m)[:, 0:C],
                            [(lhs[:, c, m * P:(m + 1) * P], rhs[:, c, :]) for c in range(KC)]).then_inc(chain_pe, 1)

            pe.wait_ge(chain_act, 1)
            pe.wait_ge(chain_dve, 1)
            pe.wait_ge(wvT_kept, 1)
            pe.wait_ge(wa_landed[0], 16)
            chain(2, gram, wk_a_sb)
            w_transposes(0)
            w_transposes(1)
            pe.wait_ge(chain_act, 2)
            pe.wait_ge(chain_dve, 2)
            pe.wait_ge(wa_landed[1], 16)
            chain(0, wq_a_sb, gram_wk)
            for k in range(2, 6):
                w_transposes(k)
            pe.wait_ge(soft_dve, 5)
            pe.wait_ge(wa_landed[3], 16)
            chain(2, attn_a, wo_a_sb)
            w_transposes(6)
            w_transposes(7)
            pe.wait_ge(chain_act, 3)
            pe.wait_ge(chain_dve, 3)
            chain(0, wvT_a, attn_wo)
            for k in range(8, 12):
                w_transposes(k)
            pe.wait_ge(chain_act, 4)
            pe.wait_ge(chain_dve, 4)
            for j in range(4):
                for t in (2 * j, 2 * j + 1):
                    tok = slice(t * P, (t + 1) * P)
                    last = product(bank(j)[:, (t % 2) * C:(t % 2 + 1) * C],
                                   [pr for c in range(KC) for pr in
                                    three((xnT_hi[:, c, tok], xnT_lo[:, c, tok]), (mix_hi[:, c, :], mix_lo[:, c, :]))])
                last.then_inc(mixed_done, 1)

            pe.wait_ge(wT_lo_done, 12)
            for hf in range(2):
                x_transposes(1, hf, 4)

            def gate_up(n):
                hf, ft = n // NF, n % NF
                if ft == 0:
                    pe.wait_ge(xT_lo_done, 4 + 2 * hf + 2)
                if n >= 2:
                    pe.wait_ge(h_done, n - 1)
                if n == 0:
                    pe.wait_ge(x_added, 4)
                tok = slice(hf * BANK, (hf + 1) * BANK)
                for half in range(2):
                    ft_s = slice(half * F + ft * P, half * F + (ft + 1) * P)
                    last = product(bank(2 * (n % 2) + half),
                                   [pr for c in range(KC) for pr in
                                    three((wguT_hi[:, c, ft_s], wguT_lo[:, c, ft_s]),
                                          (xnT_hi[:, c, tok], xnT_lo[:, c, tok]))])
                last.then_inc(gate_up_done, 1)

            def down(j):
                hf = j // 2
                pe.wait_ge(h_lo_done, NF * (hf + 1))
                if j == 0:
                    pe.wait_ge(gam_done, 1)
                for t in (2 * j, 2 * j + 1):
                    tok = slice((t % 4) * P, (t % 4 + 1) * P)
                    last = product(bank(4 + j)[:, (t % 2) * C:(t % 2 + 1) * C],
                                   [pr for i in range(NF) for pr in
                                    three((hT_hi[:, hf * NF + i, tok], hT_lo[:, hf * NF + i, tok]),
                                          (wdnT_hi[:, i, :], wdnT_lo[:, i, :]))])
                last.then_inc(down_done, 1)

            for n in range(2 * NF):
                gate_up(n)
                if n == 8:
                    pe.wait_ge(abs_done, 2)
                    nc.tensor.matmul(bank(4)[:, 0:2], ones[:], abs_sum, start=True, stop=True)\
                      .then_inc(gam_sum_done, 1)
                if n == 10:
                    down(0)
                if n == 12:
                    down(1)
            down(2)
            x_transposes(2, 0, 0)
            down(3)
            x_transposes(2, 1, 0)

            def project(split_done, value, hi, lo, half):
                pe.wait_ge(split_done, value)
                tok = slice(half * BANK, (half + 1) * BANK)
                product(bank(7), [pr for c in range(KC) for pr in
                                  three((hi[:, c, :], lo[:, c, :]), (xnT_hi[:, c, tok], xnT_lo[:, c, tok]))])\
                    .then_inc(misc_done, 1)

            pe.wait_ge(xT_lo_done, 12)
            for half in range(2):
                if half:
                    pe.wait_ge(raw_done, 1)
                project(wk_split, 1, wk_hi, wk_lo, half)
            for half in range(2):
                pe.wait_ge(raw_done, 2 + half)
                project(wq_split[0], 1, wq_hi[0], wq_lo[0], half)
            pe.wait_ge(wv_lo_done, 1)
            for t in range(NT):
                if t >= 3:
                    pe.wait_ge(v_lo_done, t - 2)
                tok = slice(t * P, (t + 1) * P)
                product(bank(4 + t % 3), [pr for c in range(KC) for pr in
                                          three((xnT_hi[:, c, tok], xnT_lo[:, c, tok]), (wv_hi[:, c, :], wv_lo[:, c, :]))])\
                    .then_inc(v_done, 1)
            pe.wait_ge(tern_done, 2)
            for q in range(4):
                dst = bank(q).bitcast(F16)
                for b in range(8):
                    src = tern[:, 0, b * C + q * P:b * C + (q + 1) * P] if q < 2 else \
                        tern[:, 1, (b % 2) * F + (4 * (q - 2) + b // 2) * P:(b % 2) * F + (4 * (q - 2) + b // 2 + 1) * P]
                    last = nc.tensor.transpose(dst[:, b * P:(b + 1) * P], src, identh[:])
                last.then_inc(ternT_done, 1)
            pe.wait_ge(v_lo_done, NT)
            pe.wait_ge(ternT_kept, 4)

            def scores(g, kind, k, par):
                p, i, a = unit(k)
                n = 32 * g + k
                if k == 0:
                    pe.wait_ge(prod_lo_done, 3 * g + 1)
                    pe.wait_ge(q_landed[0], 32 * g + 32)
                    pe.wait_ge(prod_hi_done, 3 * g + 2)
                if k == 16:
                    pe.wait_ge(q_landed[1], 32 * g + 32)
                    pe.wait_ge(prod_hi_done, 3 * g + 3)
                if not (kind == "first" and k < 2):
                    pe.wait_ge(exp_done, n - 1)
                q = q_st[p][a][:, i * P:(i + 1) * P]
                width = (i + 1) * P
                for c0 in range(0, width, BANK):
                    w = min(width - c0, BANK)
                    cols = slice(c0, c0 + max(w, 256))
                    dst = bank((k % 2) * 2 + c0 // BANK)[:, 0:max(w, 256)]
                    nc.tensor.matmul(dst, q, k_hh[par][:, cols], start=True, stop=False)
                    if c0 + w == width:
                        nc.tensor.matmul(dst[:, w - P:w], identb[:], maskb[:], start=False, stop=False,
                                         skip_group_check=True)
                    last = nc.tensor.matmul(dst, q, k_ll[par][:, cols], start=False, stop=True)
                last.then_inc(scores_done, 1)

            def probs_transposes(g, kind, k):
                p, i, a = unit(k)
                pe.wait_ge(exp_done, 32 * g + k + 1)
                for c in range(i // 4 + 1):
                    q = chunks_to(k) + c
                    if not (kind == "first" and q in (0, 1)):
                        pe.wait_ge(pT_lo_done, 48 * g + q - 1)
                    for j in range(4 * c, min(4 * c + 4, i + 1)):
                        last = nc.tensor.transpose(bank(4 + q % 2)[:, (j % 4) * P:(j % 4 + 1) * P],
                                                   probs[k % 2][:, j * P:(j + 1) * P], identf[:])
                    last.then_inc(pT_done, 1)

            def pv(g, kind, m, piece):
                s, half = 4 * g + m, m % 2
                last_j = 4 * half + 3
                if piece == 0:
                    pe.wait_ge(pT_lo_done, 48 * g + chunks_to(8 * m + 8))
                    if m == -1:
                        pe.wait_ge(vg_done, g)
                    else:
                        pe.wait_ge(vg_done, g + 1)
                    if not (kind == "first" and m == 0):
                        pe.wait_ge(o_done, s)
                def passes(j, parts):
                    off = max(0, j - 4 * half) * P
                    for v, pt, start, stop in parts:
                        for a in range(2):
                            last = nc.tensor.matmul(bank(6)[64 * a:64 * a + 64, off:BANK], v[:, j, :],
                                                    pt[a][half][:, j, off:BANK], start=start, stop=stop,
                                                    skip_group_check=True)
                    return last
                for j in (2 * piece, 2 * piece + 1):
                    parts = [(vg_hi, pT_hi, j == 0, False), (vg_hi, pT_lo, False, False)]
                    if j:
                        parts.append((vg_lo, pT_hi, False, False))
                    passes(j, parts)
                if 2 * piece + 1 == last_j:
                    passes(0, [(vg_lo, pT_hi, False, True)]).then_inc(pv_done, 1)

            def misc_emptied(g, kind, name):
                half_or_m = int(name[-1])
                if name[:2] == "q1":
                    pe.wait_ge(raw_done, 6 * g + 5 + half_or_m)
                elif name[:2] == "k_":
                    pe.wait_ge(raw_done, 6 * g + 7 + half_or_m)
                elif name[:2] == "q0":
                    pe.wait_ge(raw_done, 6 * g + 9 + half_or_m)
                elif name[:2] == "wo":
                    pe.wait_ge(x_added, 8 + 4 * (g - 1) + half_or_m + 1)
                else:
                    pe.wait_ge(recipT_done, 4 * g + (half_or_m + 1) % 4)

            def misc_free(g, kind, name):
                before = jobs(kind).index(name) - 1
                if before >= 0:
                    misc_emptied(g, kind, jobs(kind)[before])
                elif kind == "first":
                    pe.wait_ge(raw_done, FIRST_JOBS)
                else:
                    pe.wait_ge(recipT_done, 4 * g - 1)

            def recip_transposes(s):
                pe.wait_ge(recip_b_done, s + 1)
                for i in range(4):
                    last = nc.tensor.transpose(bank(7)[:, i * P:(i + 1) * P], recip_b[:, i, :], identf[:])
                last.then_inc(misc_done, 1)

            def out_project(g, j):
                if j == 0:
                    pe.wait_ge(o_lo_done, 4 * g + 4)
                    pe.wait_ge(wo_split, g + 1)
                for t in (2 * j, 2 * j + 1):
                    tok = slice(t * P, (t + 1) * P)
                    last = product(bank(7)[:, (t % 2) * C:(t % 2 + 1) * C],
                                   [pr for p in range(2) for pr in
                                    three((oT_hi[:, p, tok], oT_lo[:, p, tok]), (wo_hi[:, p, :], wo_lo[:, p, :]))])
                last.then_inc(misc_done, 1)

            def group(g, kind, par):
                for k in range(UNITS):
                    scores(g, kind, k, par)
                    if not (kind == "first" and k < LAG):
                        probs_transposes(g, kind, k - LAG)
                    piece, m = k % 8 - 3, k // 8 - 1
                    if 0 <= piece < 2 + 2 * (m % 2) and not (kind == "first" and m == -1):
                        pv(g, kind, m, piece)
                    job = MISC.get(k)
                    if job and has(kind, job):
                        misc_free(g, kind, job)
                        last_char = int(job[-1])
                        if job[:2] == "q1":
                            project(wq_split[1], g + 1, wq_hi[1], wq_lo[1], last_char)
                        elif job[:2] == "k_":
                            project(wk_split, g + 2, wk_hi, wk_lo, last_char)
                        elif job[:2] == "q0":
                            project(wq_split[0], g + 2, wq_hi[0], wq_lo[0], last_char)
                        elif job[:2] == "wo":
                            out_project(g - 1, last_char)
                        else:
                            recip_transposes(4 * g + (-1 if last_char == 3 else last_char))

            run_groups(pe, group)
            g = NG
            probs_transposes(g, "mid", -2)
            probs_transposes(g, "mid", -1)
            pe.wait_ge(recipT_done, 4 * NG - 1)
            recip_transposes(4 * NG - 1)
            for piece in range(4):
                pv(g, "mid", -1, piece)
            for j in range(4):
                if j == 0:
                    pe.wait_ge(recipT_done, 4 * NG)
                else:
                    pe.wait_ge(x_added, 8 + 4 * (NG - 1) + j)
                out_project(NG - 1, j)

            for hf in range(2):
                x_transposes(3, hf, 0)
            pe.wait_ge(xT_lo_done, 16)

            def fc(t):
                if t >= 2:
                    pe.wait_ge(gelu_done, t - 1)
                tok = slice(t * P, (t + 1) * P)
                for n in range(2):
                    cols = slice(n * BANK, (n + 1) * BANK)
                    last = product(bank(2 * (t % 2) + n), [(yT[:, c, tok], fcT[:, c, cols])
                                                           for c in range(KC) for yT in (yT_hi, yT_lo)])
                last.then_inc(fc_done, 1)

            def z_transposes(t):
                pe.wait_ge(z_done, 2 * t + 2)
                if t >= 1:
                    pe.wait_ge(zT_lo_done, t)
                for i in range(NF):
                    last = nc.tensor.transpose(bank(4, 2)[:, i * P:(i + 1) * P], z[:, t % 2, i * P:(i + 1) * P],
                                               identf[:])
                last.then_inc(zT_done, 1)

            def pj(t):
                pe.wait_ge(zT_lo_done, t + 1)
                if t >= 2:
                    pe.wait_ge(result_done, t - 1)
                product(bank(6 + t % 2)[:, 0:C], [(zT[:, t % 2, i, :], pjT[:, i, :])
                                                  for i in range(NF) for zT in (zT_hi, zT_lo)]).then_inc(pj_done, 1)

            fc(0)
            for t in range(NT):
                if t + 1 < NT:
                    fc(t + 1)
                z_transposes(t)
                if t >= 1:
                    pj(t - 1)
            pj(NT - 1)


_INS = ["L0_attn_x", "L0_attn_Wq", "L0_attn_Wk", "L0_attn_Wv", "L0_attn_Wo", "L0_ffn_w_gate_up", "L0_ffn_w_down",
        "L1_attn_wq", "L1_attn_wk", "L1_attn_wv", "L1_attn_wo", "L1_ffn_w_fc", "L1_ffn_w_proj"]


def rope_tables(tokens, head, heads):
    import numpy as np

    freqs = (np.float32(10000.0) ** (-np.arange(0, head, 2, dtype=np.float32) / np.float32(head))).astype(np.float32)
    theta = np.outer(freqs, np.arange(tokens, dtype=np.float32)).astype(np.float32)
    cos = np.cos(theta).astype(np.float32)
    sin = np.sin(theta).astype(np.float32)
    return (np.ascontiguousarray(np.concatenate([cos, cos] * heads)),
            np.ascontiguousarray(np.concatenate([-sin, sin] * heads)))


def kernel(**inputs):
    import numpy as np
    import concourse.bacc as bacc
    from concourse import mybir as _mybir
    from concourse.bass_utils import run_bass_kernel_spmd

    nc = bacc.Bacc("TRN2", target_bir_lowering=False, num_devices=1)
    cos, sin = rope_tables(1024, 64, 2)
    arrays = {name: np.ascontiguousarray(inputs[name]) for name in _INS}
    arrays["rope_cos"], arrays["rope_sin"] = cos, sin
    args = [nc.dram_tensor(n, a.shape, _mybir.dt.from_np(a.dtype), kind="ExternalInput").ap() for n, a in arrays.items()]
    out = nc.dram_tensor("out_0", (1, 1024, 256), F32, kind="ExternalOutput").ap()
    transformer_program(nc, *args, out)
    r = run_bass_kernel_spmd(nc, [arrays], core_ids=[0])
    return r.results[0]["out_0"]
```

```python
from contextlib import ExitStack

import concourse.bass as bass
from concourse import mybir

F32 = mybir.dt.float32
F32R = mybir.dt.float32r
F16 = mybir.dt.float16
BF16 = mybir.dt.bfloat16
ALU = mybir.AluOpType
ACT = mybir.ActivationFunctionType
AX = mybir.AxisListType

P = 128
BANK = 512
LN_EPS = 1e-5
BIT_EPS = 1e-6
Q_B = 128.0
MASKED = -1e30


def transformer_program(nc, x_in, wq_a, wk_a, wv_a, wo_a, w_gate_up, w_down,
                        wq_b, wk_b, wv_b, wo_b, w_fc, w_proj, cos_in, sin_in, out):
    T, C = x_in.shape[1], x_in.shape[2]
    NT = T // P
    KC = C // P
    F = w_down.shape[1]
    NF = F // P
    HEAD = 64
    NG = wk_b.shape[1] // HEAD
    NH = wq_b.shape[1] // HEAD
    assert NH == 4 * NG and T == 1024 and C == 256 and F == 1024

    base = (nc.sbuf_base + 31) // 32 * 32

    def sb(name, kb, shape, dt):
        return nc.alloc_sbuf_tensor_at(name, [P] + shape, dt, offset=base + int(kb * 1024))

    x = sb("x", 0, [NT, C], F32)
    xnT_hi = sb("xnT_hi", 8, [KC, T], F32R)
    xnT_lo = sb("xnT_lo", 16, [KC, T], F32R)
    identf = sb("identf", 24, [P], F32)
    identh = sb("identh", 24.5, [P], F16)
    identb = sb("identb", 24.75, [P], BF16)
    maskb = sb("maskb", 25, [P], BF16)
    stats = sb("stats", 25.25, [6 * NT], F32)
    moments = sb("moments", 25.4375, [4, 2 * NT], F32)
    small = sb("small", 25.6875, [64], F32)
    ones = sb("ones", 207, [P], F32)
    xn = sb("xn", 26, [NT, C], F32)
    wq_a_sb = sb("wq_a_sb", 34, [KC, C], F32)
    wk_a_sb = sb("wk_a_sb", 36, [KC, C], F32)
    wv_a_sb = sb("wv_a_sb", 38, [KC, C], F32)
    wo_a_sb = sb("wo_a_sb", 40, [KC, C], F32)
    wvT_a = sb("wvT_a", 42, [KC, C], F32)
    gram = sb("gram", 44, [KC, C], F32)
    gram_wk = sb("gram_wk", 46, [KC, C], F32)
    attn_a = sb("attn_a", 48, [KC, C], F32)
    attn_wo = sb("attn_wo", 50, [KC, C], F32)
    mix_hi = sb("mix_hi", 52, [KC, C], F32R)
    mix_lo = sb("mix_lo", 54, [KC, C], F32R)
    wdn_nat = sb("wdn_nat", 56, [KC, F], F32)
    wgu_nat = sb("wgu_nat", 64, [2 * NF, C], F32)
    wguT_hi = sb("wguT_hi", 80, [KC, 2 * F], F32R)
    wguT_lo = sb("wguT_lo", 96, [KC, 2 * F], F32R)
    wdnT_hi = sb("wdnT_hi", 112, [NF, C], F32R)
    wdnT_lo = sb("wdnT_lo", 120, [NF, C], F32R)
    silu = sb("silu", 128, [2, BANK], F32)
    h32 = sb("h32", 132, [3, BANK], F32)
    hT_hi = sb("hT_hi", 138, [2 * NF, BANK], F32R)
    hT_lo = sb("hT_lo", 170, [2 * NF, BANK], F32R)
    wfc_nat = sb("wfc_nat", 64, [NF, C], F32)
    wpj_nat = sb("wpj_nat", 72, [KC, F], F32)
    above = sb("above", 202, [2 * F], F16)
    tern = sb("tern", 56, [2, 2 * F], F16)
    fcT = sb("fcT", 96, [KC, F], F16)
    pjT = sb("pjT", 100, [NF, C], F16)
    cosT = sb("cosT", 34, [T], F32)
    sinT = sb("sinT", 38, [T], F32)
    wv_nat = sb("wv_nat", 42, [KC, NG * HEAD], F32)
    wv_hi = sb("wv_hi", 46, [KC, NG * HEAD], F32R)
    wv_lo = sb("wv_lo", 50, [KC, NG * HEAD], F32R)
    v_hi = sb("v_hi", 80, [NT, NG * HEAD], F16)
    v_lo = sb("v_lo", 88, [NT, NG * HEAD], F16)
    wk_nat = sb("wk_nat", 202, [KC, P], F32)
    wq_nat = [sb(f"wq_nat{p}", 203 + p, [KC, P], F32) for p in range(2)]
    wo_nat = sb("wo_nat", 205, [2, C], F32)
    wk_hi = sb("wk_hi", 112, [KC, P], F32R)
    wk_lo = sb("wk_lo", 113, [KC, P], F32R)
    wq_hi = [sb(f"wq_hi{p}", 114 + 2 * p, [KC, P], F32R) for p in range(2)]
    wq_lo = [sb(f"wq_lo{p}", 115 + 2 * p, [KC, P], F32R) for p in range(2)]
    wo_hi = sb("wo_hi", 118, [2, C], F32R)
    wo_lo = sb("wo_lo", 120, [2, C], F32R)
    vg_hi = sb("vg_hi", 122, [NT, HEAD], F16)
    vg_lo = sb("vg_lo", 123, [NT, HEAD], F16)
    wk0_hi = sb("wk0_hi", 64, [KC, P], F32R)
    wk0_lo = sb("wk0_lo", 65, [KC, P], F32R)
    wq0_hi = sb("wq0_hi", 66, [KC, P], F32R)
    wq0_lo = sb("wq0_lo", 67, [KC, P], F32R)
    k_hh = [sb(f"k_hh{b}", 138 + 8 * b, [T], F32R) for b in range(2)]
    k_ll = [sb(f"k_ll{b}", 142 + 8 * b, [T], F32R) for b in range(2)]
    q_st = [[sb(f"q_st{p}{a}", 154 + 8 * p + 4 * a, [T], F32R) for a in range(2)] for p in range(2)]
    raw = [sb(f"raw{b}", 170 + 4 * b, [T], F32) for b in range(2)]
    swapped = sb("swapped", 178, [T], F32)
    roped = sb("roped", 182, [T], F32)
    k0_roped = sb("k0_roped", 186, [T], F32)
    k0_swapped = sb("k0_swapped", 190, [T], F32)
    pT_hi = [[sb("pT_hi00", 186, [4, BANK], F16), sb("pT_hi01", 26, [8, BANK], F16)],
             [sb("pT_hi10", 190, [4, BANK], F16), sb("pT_hi11", 104, [8, BANK], F16)]]
    pT_lo = [[sb("pT_lo00", 194, [4, BANK], F16), sb("pT_lo01", 128, [8, BANK], F16)],
             [sb("pT_lo10", 198, [4, BANK], F16), sb("pT_lo11", 42, [8, BANK], F16)]]
    recip_b = sb("recip_b", 50, [4, P], F32)
    recipT = sb("recipT", 52, [BANK], F32)
    o32 = sb("o32", 54, [BANK], F32)
    probs = [sb(f"probs{b}", 56 + 4 * b, [T], F32) for b in range(2)]
    oT_hi = sb("oT_hi", 64, [2, T], F32R)
    oT_lo = sb("oT_lo", 72, [2, T], F32R)
    y = sb("y", 26, [NT, C], F32)
    yT_hi = sb("yT_hi", 34, [KC, T], F16)
    yT_lo = sb("yT_lo", 38, [KC, T], F16)
    gelu = sb("gelu", 138, [2, F], F32)
    z = sb("z", 146, [2, F], F32)
    zT_hi = sb("zT_hi", 154, [2, NF, P], F16)
    zT_lo = sb("zT_lo", 158, [2, NF, P], F16)
    square = sb("square", 162, [F], BF16)
    bit = sb("bit", 164, [11, NT], F32)

    def col(i, n=1):
        return small[:, i:i + n]
    neg_half = col(0)
    abs_sum = col(1, 2)
    gam = col(3, 2)
    thr = col(5, 2)
    nthr = col(7, 2)
    ngam = col(9, 2)
    wv_max = col(11)
    v_inv = col(13)
    v_scale = col(14)
    wv_all = col(15)
    nmax = small[:, 16:20]
    s_nmax = col(20, 2)
    s_scaled = col(22, 2)
    s_sum = col(24, 2)
    s_rec = col(26, 2)
    lsum = small[:, 28:44].rearrange("p (s u) -> p s u", s=2)
    lrec = small[:, 44:60].rearrange("p (s u) -> p s u", s=2)

    def mean_of(st, i):
        return moments[:, st, 2 * i:2 * i + 1]

    with ExitStack() as ctx:
        PS = ctx.enter_context(nc.psum_tensor("PS", [P, 8 * BANK], F32))

        def bank(b, n=1):
            return PS[:, b * BANK:(b + n) * BANK]

        def two_chunks(b):
            return bank(b, 2).rearrange("p (m n) -> p m n", m=2)[:, :, 0:C]

        def sem(name):
            return ctx.enter_context(nc.semaphore(name))

        x_landed = [sem(f"x_landed{j}") for j in range(NT // 2)]
        wa_landed = [sem(f"wa_landed{j}") for j in range(4)]
        wgu_landed = [sem(f"wgu_landed{j}") for j in range(2)]
        wdn_landed = sem("wdn_landed")
        tern_landed = [sem(f"tern_landed{j}") for j in range(2)]
        rope_landed = sem("rope_landed")
        wv_landed = sem("wv_landed")
        wk_landed = sem("wk_landed")
        wq_landed = [sem(f"wq_landed{p}") for p in range(2)]
        wo_landed = sem("wo_landed")
        out_stored = sem("out_stored")
        const_step = sem("const_step")
        const_ready = sem("const_ready")
        stats_done = sem("stats_done")
        moments_done = sem("moments_done")
        var_eps_done = sem("var_eps_done")
        rstd_done = sem("rstd_done")
        xn_done = sem("xn_done")
        xT_done = sem("xT_done")
        xT_hi_done = sem("xT_hi_done")
        xT_lo_done = sem("xT_lo_done")
        x_added = sem("x_added")
        wvT_done, wvT_kept = sem("wvT_done"), sem("wvT_kept")
        chain_pe = sem("chain_pe")
        chain_act = sem("chain_act")
        chain_dve = sem("chain_dve")
        soft_dve = sem("soft_dve")
        soft_act = sem("soft_act")
        mixed_done = sem("mixed_done")
        wT_done, wT_hi_done, wT_lo_done = sem("wT_done"), sem("wT_hi_done"), sem("wT_lo_done")
        gate_up_done, silu_done, h_done = sem("gate_up_done"), sem("silu_done"), sem("h_done")
        h_hi_done, h_lo_done, down_done = sem("h_hi_done"), sem("h_lo_done"), sem("down_done")
        abs_done, gam_sum_done, gam_done = sem("abs_done"), sem("gam_sum_done"), sem("gam_done")
        above_done, tern_done = sem("above_done"), sem("tern_done")
        ternT_done, ternT_kept = sem("ternT_done"), sem("ternT_kept")
        wv_max_done, wv_all_done, v_scale_done = sem("wv_max_done"), sem("wv_all_done"), sem("v_scale_done")
        wv_hi_done, wv_lo_done = sem("wv_hi_done"), sem("wv_lo_done")
        v_done, v_hi_done, v_lo_done = sem("v_done"), sem("v_hi_done"), sem("v_lo_done")
        raw_done, swap_landed, rope_mul = sem("raw_done"), sem("swap_landed"), sem("rope_mul")
        k0_swap_landed = [sem(f"k0_swap_landed{h}") for h in range(2)]
        k0_mul, k0_roped_done, k0_lo_done = sem("k0_mul"), sem("k0_roped_done"), sem("k0_lo_done")
        q0_swap_landed, q0_mul, q0_roped_done = sem("q0_swap_landed"), sem("q0_mul"), sem("q0_roped_done")
        q0_half_lo_done, q0_lo_done = sem("q0_half_lo_done"), sem("q0_lo_done")
        first_hi_done, q0_landed = sem("first_hi_done"), sem("q0_landed")
        low_q_done = sem("low_q_done")
        roped_done, prod_hi_done, prod_lo_done = sem("roped_done"), sem("prod_hi_done"), sem("prod_lo_done")
        q_landed = [sem(f"q_landed{p}") for p in range(2)]
        wk_split, wo_split = sem("wk_split"), sem("wo_split")
        wq_split = [sem(f"wq_split{p}") for p in range(2)]
        split_hi = sem("split_hi")
        scores_done, nmax_done, exp_done = sem("scores_done"), sem("nmax_done"), sem("exp_done")
        pT_done, pT_hi_done, pT_lo_done = sem("pT_done"), sem("pT_hi_done"), sem("pT_lo_done")
        recip_done, recip_b_done, recipT_done = sem("recip_done"), sem("recip_b_done"), sem("recipT_done")
        vg_done, pv_done = sem("vg_done"), sem("pv_done")
        o_done, o_hi_done, o_lo_done = sem("o_done"), sem("o_hi_done"), sem("o_lo_done")
        misc_done = sem("misc_done")
        bit_step = sem("bit_step")
        y_done = sem("y_done")
        fc_done, gelu_done = sem("fc_done"), sem("gelu_done")
        z_mean_done, z_centred, z_squares_done = sem("z_mean_done"), sem("z_centred"), sem("z_squares_done")
        z_var_done, z_rstd_done, z_done = sem("z_var_done"), sem("z_rstd_done"), sem("z_done")
        zT_done, zT_hi_done, zT_lo_done = sem("zT_done"), sem("zT_hi_done"), sem("zT_lo_done")
        pj_done, result_done = sem("pj_done"), sem("result_done")

        x_dram = x_in.rearrange("a (i p) c -> p (a i) c", p=P)
        out_dram = out.rearrange("a (i p) c -> p (a i) c", p=P)

        def rows(w):
            return w.rearrange("(c p) n -> p c n", p=P)

        LAG = 2
        UNITS = 32

        def chunks_to(k):
            if k < 0:
                return chunks_to(k + UNITS) - 48
            kk = k % 16
            return 24 * (k // 16) + (kk if kk < 8 else 8 + 2 * (kk - 8))

        def unit(k):
            kk = k % 16
            return (k // 16) % 2, kk // 2, kk % 2

        MISC = {0: "f1_0", 1: "f1_1", 2: "rl3", 4: "k_0", 8: "k_1", 10: "wo_0", 11: "wo_1", 13: "wo_2",
                14: "rl0", 15: "wo_3", 16: "q0_0", 17: "q0_1", 20: "rl1", 23: "q1_0", 25: "q1_1", 26: "rl2"}

        AT = {"split_wk": 2, "split_wq0": 6, "split_wo": 5, "split_wq1": 17, "values": 9, "high_f1": 10,
              "high_q1": 4, "high_k": 16, "high_q0": 23, "recips": 0, "scale_o": 7, "high_o": 7, "pv": 3}

        def has(kind, name):
            if name[:2] == "f1":
                return kind == "first"
            if kind == "first" and (name == "rl3" or name.startswith("wo")):
                return False
            return not (kind == "last" and name[:2] in ("k_", "q0", "q1"))

        def jobs(kind):
            return [n for _, n in sorted(MISC.items()) if has(kind, n)]

        FIRST_JOBS = 4

        def misc_before(g, kind):
            return FIRST_JOBS if kind == "first" else FIRST_JOBS + len(jobs("first")) + (g - 1) * len(jobs("mid"))

        def misc_index(g, kind, name):
            return misc_before(g, kind) + jobs(kind).index(name)

        MISC_TAIL = misc_before(NG - 1, "last") + len(jobs("last"))

        def run_groups(eng, emit):
            emit(0, "first", 0)
            with eng.Fori(0, (NG - 2) // 2) as turn:
                emit(turn * 2 + 1, "mid", 1)
                emit(turn * 2 + 2, "mid", 0)
            emit(NG - 1, "last", (NG - 1) % 2)

        HALVES = [slice(0, BANK), slice(BANK, 2 * BANK)]
        V_BANK = [0, 1, 6, 7, 0, 1, 2, 3]

        block = ctx.enter_context(nc.Block())

        @block.sync
        def _(sp):
            for j in range(NT // 2):
                sp.dma_start(x[:, 2 * j:2 * j + 2, :], x_dram[:, 2 * j:2 * j + 2, :]).then_inc(x_landed[j], 16)
            for j in range(2):
                sp.dma_start(wgu_nat[:, NF * j:NF * (j + 1), :],
                             rows(w_gate_up)[:, NF * j:NF * (j + 1), :]).then_inc(wgu_landed[j], 16)
            sp.dma_start(wdn_nat[:], rows(w_down)).then_inc(wdn_landed, 16)
            sp.wait_ge(wT_done, 8)
            sp.dma_start(wfc_nat[:], rows(w_fc)).then_inc(tern_landed[0], 16)
            sp.dma_start(wpj_nat[:], rows(w_proj)).then_inc(tern_landed[1], 16)
            sp.wait_ge(mixed_done, 4)
            sp.dma_start(cosT[:], cos_in).then_inc(rope_landed, 16)
            sp.dma_start(sinT[:], sin_in).then_inc(rope_landed, 16)
            sp.dma_start(wv_nat[:], rows(wv_b)).then_inc(wv_landed, 16)

            def load_wk(g):
                for half in range(2):
                    sp.dma_start(wk_nat[:, :, HEAD * half:HEAD * (half + 1)],
                                 rows(wk_b)[:, :, bass.ds(g * HEAD, HEAD)]).then_inc(wk_landed, 16)

            def load_wq(g, p):
                sp.dma_start(wq_nat[p][:], rows(wq_b)[:, :, bass.ds(g * 2 * P + p * P, P)]).then_inc(wq_landed[p], 16)

            def load_wo(g):
                for p in range(2):
                    sp.dma_start(wo_nat[:, p, :], wo_b[bass.ds(g * 2 * P + p * P, P), :]).then_inc(wo_landed, 16)

            sp.wait_ge(tern_done, 2)
            load_wk(0)
            load_wq(0, 0)
            load_wq(0, 1)

            def swap_halves(dst, src, tok, landed):
                for d, s in ((0, 32), (32, 0), (64, 96), (96, 64)):
                    sp.dma_start(dst[d:d + 32, tok], src[s:s + 32, tok]).then_inc(landed, 16)

            def swap(r, par):
                sp.wait_ge(raw_done, 2 * r + 2)
                sp.wait_ge(roped_done, r)
                swap_halves(swapped, raw[par], slice(0, T), swap_landed)

            def spread_low(p, par, tok, landed):
                sp.dma_start(q_st[p][0][64:128, tok].bitcast(F32), raw[par][0:64, tok]).then_inc(landed, 16)
                sp.dma_start(q_st[p][1][0:64, tok].bitcast(F32), raw[par][64:128, tok]).then_inc(landed, 16)

            def spread_lo(r, p, par):
                sp.wait_ge(prod_lo_done, r + 1)
                spread_low(p, par, slice(0, T), q_landed[p])

            for half in range(2):
                sp.wait_ge(raw_done, 2 * half + 1)
                swap_halves(k0_swapped, raw[0], HALVES[half], k0_swap_landed[half])
                sp.wait_ge(raw_done, 2 * half + 2)
                swap_halves(swapped, raw[1], HALVES[half], (q0_swap_landed, swap_landed)[half])
            sp.wait_ge(q0_lo_done, 1)
            spread_low(0, 1, HALVES[0], q0_landed)
            sp.wait_ge(prod_lo_done, 2)
            spread_low(0, 1, HALVES[1], q_landed[0])

            def group(g, kind, par):
                if kind != "last":
                    sp.wait_ge(wk_split, g + 1)
                    load_wk(g + 1)
                if kind != "first":
                    sp.wait_ge(misc_done, misc_before(g, kind))
                    load_wo(g - 1)
                if kind != "last":
                    sp.wait_ge(wq_split[0], g + 1)
                    load_wq(g + 1, 0)
                    sp.wait_ge(wq_split[1], g + 1)
                    load_wq(g + 1, 1)
                if kind == "first":
                    swap(2, 0)
                if kind != "last":
                    swap(3 * g + 3, 1 - par)
                spread_lo(3 * g + 2, 1, par)
                if kind != "last":
                    swap(3 * g + 4, par)
                    spread_lo(3 * g + 4, 0, par)
                    swap(3 * g + 5, 1 - par)

            run_groups(sp, group)
            sp.wait_ge(wo_split, NG - 1)
            load_wo(NG - 1)
            for t in range(NT):
                sp.wait_ge(result_done, t + 1)
                sp.dma_start(out_dram[:, t, :], x[:, t, :]).then_inc(out_stored, 16)
            sp.wait_ge(out_stored, 16 * NT)

        @block.gpsimd
        def _(pool):
            nc.gpsimd.memset(identf[:], 0.0).then_inc(const_step, 1)
            nc.gpsimd.memset(roped[:, 0:P], 0.0).then_inc(const_step, 1)
            pool.wait_ge(const_step, 2)
            nc.gpsimd.affine_select(out=identf[:], in_=identf[:], compare_op=ALU.not_equal, fill=1.0, base=0,
                                    pattern=[[-1, P]], channel_multiplier=1).then_inc(const_step, 1)
            nc.gpsimd.affine_select(out=roped[:, 0:P], in_=roped[:, 0:P], compare_op=ALU.is_ge, fill=MASKED,
                                    base=0, pattern=[[-1, P]], channel_multiplier=1).then_inc(const_step, 1)
            nc.gpsimd.memset(neg_half, -0.5)
            nc.gpsimd.memset(ones[:], 1.0)
            pool.wait_ge(const_step, 4)
            nc.gpsimd.tensor_copy(identb[:], identf[:])
            nc.gpsimd.tensor_copy(identh[:], identf[:])
            nc.gpsimd.tensor_copy(maskb[:], roped[:, 0:P]).then_inc(const_ready, 1)
            pool.wait_ge(const_ready, 1)

            def rstd(st, i, eps):
                v = moments[:, st, 2 * i + 1:2 * i + 2]
                pool.wait_ge(moments_done, st * NT + i + 1)
                nc.gpsimd.tensor_scalar(v, v, eps, None, ALU.add).then_inc(var_eps_done, 1)
                pool.wait_ge(var_eps_done, st * NT + i + 1)
                nc.gpsimd.tensor_tensor(v, v, neg_half, ALU.pow).then_inc(rstd_done, 1)

            for i in range(NT):
                rstd(0, i, LN_EPS)
            for i in range(NT):
                rstd(1, i, LN_EPS)

            def h_low(n):
                pool.wait_ge(h_hi_done, n + 1)
                nc.gpsimd.tensor_tensor(hT_lo[:, n, :], h32[:, n % 3, :], hT_hi[:, n, :].bitcast(F32),
                                        ALU.subtract).then_inc(h_lo_done, 1)

            def split(nat, hi, lo, landed, value, done, count):
                pool.wait_ge(landed, value)
                nc.gpsimd.tensor_copy(hi[:], nat[:]).then_inc(split_hi, 1)
                pool.wait_ge(split_hi, count)
                nc.gpsimd.tensor_tensor(lo[:], nat[:], hi[:].bitcast(F32), ALU.subtract).then_inc(done, 1)

            for n in range(2 * NF):
                h_low(n)
                if n == 5:
                    pool.wait_ge(wv_max_done, 1)
                    nc.gpsimd.partition_all_reduce(wv_all, wv_max, P, bass.bass_isa.ReduceOp.max)\
                      .then_inc(wv_all_done, 1)
                if n >= 12 and n < 16:
                    rstd(2, n - 12, LN_EPS)
                if n == 12:
                    split(wk_nat, wk0_hi, wk0_lo, wk_landed, 32, wk_split, 1)
            split(wq_nat[0], wq0_hi, wq0_lo, wq_landed[0], 16, wq_split[0], 2)

            for i in range(4, NT):
                rstd(2, i, LN_EPS)
            pool.wait_ge(down_done, 4)
            split(wq_nat[1], wq_hi[1], wq_lo[1], wq_landed[1], 16, wq_split[1], 3)

            def rope(r, par, tok=slice(0, T), muls=rope_mul, swap_sem=swap_landed, done=roped_done):
                nc.gpsimd.tensor_tensor(roped[:, tok], raw[par][:, tok], cosT[:, tok], ALU.mult).then_inc(muls, 1)
                pool.wait_ge(swap_sem, r * 64)
                nc.gpsimd.tensor_tensor(swapped[:, tok], swapped[:, tok], sinT[:, tok], ALU.mult).then_inc(muls, 1)
                pool.wait_ge(muls, 2 * r)
                if isinstance(r, int) and r == 1 and done is roped_done:
                    pool.wait_ge(roped_done, 1)
                nc.gpsimd.tensor_tensor(roped[:, tok], roped[:, tok], swapped[:, tok], ALU.add).then_inc(done, 1)

            def rope_next(r, par):
                pool.wait_ge(prod_lo_done, r)
                pool.wait_ge(raw_done, 2 * r + 2)
                rope(r, par)

            def low_q(p, par, halves_done, count, done, tok=slice(0, T)):
                nc.gpsimd.tensor_tensor(raw[par][0:64, tok], roped[0:64, tok], q_st[p][0][0:64, tok].bitcast(F32),
                                        ALU.subtract).then_inc(halves_done, 1)
                pool.wait_ge(halves_done, count)
                nc.gpsimd.tensor_tensor(raw[par][64:128, tok], roped[64:128, tok],
                                        q_st[p][1][64:128, tok].bitcast(F32), ALU.subtract).then_inc(done, 1)

            def low_q_next(r, p, par, count):
                pool.wait_ge(prod_hi_done, r + 1)
                low_q(p, par, low_q_done, count, prod_lo_done)
                pool.wait_ge(prod_lo_done, r + 1)

            def low_k(r, slot):
                pool.wait_ge(prod_hi_done, r + 1)
                nc.gpsimd.tensor_tensor(k_ll[slot][:], roped[:], k_hh[slot][:].bitcast(F32),
                                        ALU.subtract).then_inc(prod_lo_done, 1)

            def low_o(s, m):
                p, half = m // 2, m % 2
                pool.wait_ge(o_hi_done, s + 1)
                nc.gpsimd.tensor_tensor(oT_lo[:, p, half * BANK:(half + 1) * BANK], o32[:],
                                        oT_hi[:, p, half * BANK:(half + 1) * BANK].bitcast(F32),
                                        ALU.subtract).then_inc(o_lo_done, 1)

            pool.wait_ge(rope_landed, 32)
            pool.wait_ge(down_done, 4)
            pool.wait_ge(raw_done, 2)
            rope(1, 1, HALVES[0], q0_mul, q0_swap_landed, q0_roped_done)
            pool.wait_ge(first_hi_done, 2)
            low_q(0, 1, q0_half_lo_done, 1, q0_lo_done, HALVES[0])
            pool.wait_ge(q0_lo_done, 1)
            pool.wait_ge(raw_done, 4)
            rope(1, 1, HALVES[1])
            pool.wait_ge(prod_hi_done, 2)
            pool.wait_ge(prod_lo_done, 1)
            low_q(0, 1, low_q_done, 1, prod_lo_done, HALVES[1])
            pool.wait_ge(prod_lo_done, 2)

            def group(g, kind, par):
                if kind == "first":
                    rope_next(2, 0)
                low_q_next(3 * g + 2, 1, par, 2 * g + 2)
                if kind != "first":
                    low_o(4 * g - 1, 3)
                if kind != "last":
                    rope_next(3 * g + 3, 1 - par)
                    low_k(3 * g + 3, 1 - par)
                low_o(4 * g, 0)
                if kind != "last":
                    rope_next(3 * g + 4, par)
                low_o(4 * g + 1, 1)
                if kind != "last":
                    low_q_next(3 * g + 4, 0, par, 2 * g + 3)
                    rope_next(3 * g + 5, 1 - par)
                low_o(4 * g + 2, 2)

            run_groups(pool, group)
            low_o(4 * NG - 1, 3)
            for i in range(NT):
                rstd(3, i, BIT_EPS)

            def z_mean(t):
                pool.wait_ge(gelu_done, t + 1)
                nc.gpsimd.tensor_scalar(bit[:, 9, t:t + 1], bit[:, 8, t:t + 1], -1.0 / F, None,
                                        ALU.mult).then_inc(z_mean_done, 1)

            def z_rstd(t):
                v = bit[:, 10, t:t + 1]
                pool.wait_ge(z_squares_done, t + 1)
                nc.gpsimd.tensor_scalar(v, v, 1.0 / F, BIT_EPS, ALU.mult, ALU.add).then_inc(z_var_done, 1)
                pool.wait_ge(z_var_done, t + 1)
                nc.gpsimd.tensor_tensor(v, v, neg_half, ALU.pow).then_inc(z_rstd_done, 1)

            for t in range(NT):
                z_mean(t)
                if t:
                    z_rstd(t - 1)
            z_rstd(NT - 1)

        @block.scalar
        def _(act):
            for j, (w, dst) in enumerate(((wk_a, wk_a_sb), (wq_a, wq_a_sb), (wv_a, wv_a_sb), (wo_a, wo_a_sb))):
                act.dma_start(dst[:], rows(w)).then_inc(wa_landed[j], 16)

            def x_high(st, hf, c, b):
                act.wait_ge(xT_done, 4 * st + 2 * hf + c + 1)
                dst = (yT_hi if st == 3 else xnT_hi)[:, c, hf * BANK:(hf + 1) * BANK]
                nc.scalar.copy(dst, bank(b)).then_inc(xT_hi_done, 1)

            act.wait_ge(wvT_done, 1)
            nc.scalar.copy(wvT_a[:], bank(2).rearrange("p (c n) -> p c n", c=KC)).then_inc(wvT_kept, 1)
            for hf in range(2):
                for c in range(KC):
                    x_high(0, hf, c, 4 + 2 * hf + c)

            def w_high(k):
                act.wait_ge(wT_done, k + 1)
                dst = wguT_hi[:, k % 2, (k // 2) * BANK:(k // 2 + 1) * BANK] if k < 8 else wdnT_hi[:, 2 * (k - 8):2 * (k - 7), :]
                src = bank(4 + k % 4) if k < 8 else bank(4 + k % 4).rearrange("p (i n) -> p i n", i=2)
                nc.scalar.copy(dst, src).then_inc(wT_hi_done, 1)

            act.wait_ge(chain_pe, 1)
            nc.scalar.copy(gram[:, 0, :], bank(0)[:, 0:C]).then_inc(chain_act, 1)
            act.wait_ge(chain_pe, 3)
            nc.scalar.copy(gram_wk[:, 0, :], bank(2)[:, 0:C]).then_inc(chain_act, 1)
            w_high(0)
            w_high(1)
            for m in range(KC):
                act.wait_ge(soft_dve, 2)
                nc.scalar.activation(attn_a[:, m, :], bank(m)[:, 0:C], ACT.Exp,
                                     bias=s_scaled[:, m:m + 1], scale=8 ** -0.5,
                                     accum_out=s_sum[:, m:m + 1]).then_inc(soft_act, 1)
            for k in range(2, 6):
                w_high(k)
            act.wait_ge(chain_pe, 7)
            nc.scalar.copy(attn_wo[:, 0, :], bank(2)[:, 0:C]).then_inc(chain_act, 1)
            w_high(6)
            w_high(7)
            act.wait_ge(chain_pe, 10)
            nc.scalar.copy(mix_hi[:], two_chunks(0)).then_inc(chain_act, 1)
            for k in range(8, 12):
                w_high(k)

            for hf in range(2):
                for c in range(KC):
                    x_high(1, hf, c, 4 + 2 * hf + c)
            for n in range(2 * NF):
                act.wait_ge(gate_up_done, n + 1)
                if n >= 2:
                    act.wait_ge(h_done, n - 1)
                nc.scalar.activation(silu[:, n % 2, :], bank(2 * (n % 2)), ACT.Silu).then_inc(silu_done, 1)
                if n in (5, 7):
                    m = (n - 5) // 2
                    act.wait_ge(tern_landed[m], 16)
                    if m:
                        act.wait_ge(abs_done, 1)
                    nat = (wfc_nat, wpj_nat)[m]
                    nc.scalar.activation(above[:].rearrange("p (a b) -> p a b", a=nat.shape[1]), nat[:], ACT.Abs,
                                         accum_out=abs_sum[:, m:m + 1]).then_inc(abs_done, 1)
                if n == 9:
                    act.wait_ge(wv_landed, 16)
                    nc.scalar.copy(wv_hi[:], wv_nat[:]).then_inc(wv_hi_done, 1)

            def raw_half(par, half, job, scale, guard=None, b=7):
                act.wait_ge(misc_done, job + 1)
                if half == 0 and guard is not None:
                    guard()
                nc.scalar.mul(raw[par][:, half * BANK:(half + 1) * BANK], bank(b), scale).then_inc(raw_done, 1)

            Q_SCALE = HEAD ** -0.5

            def v_high(t):
                act.wait_ge(v_done, t + 1)
                act.wait_ge(v_scale_done, 3)
                nc.scalar.activation(v_hi[:, t, :], bank(V_BANK[t]), ACT.Copy, scale=v_scale).then_inc(v_hi_done, 1)

            def k0_high(half):
                act.wait_ge((k0_roped_done, roped_done)[half], 1)
                nc.scalar.copy(k_hh[0][:, HALVES[half]], k0_roped[:, HALVES[half]])\
                  .then_inc((first_hi_done, prod_hi_done)[half], 1)

            def q0_high(half):
                act.wait_ge((q0_roped_done, roped_done)[half], 1 + half)
                nc.scalar.copy(q_st[0][0][0:64, HALVES[half]], roped[0:64, HALVES[half]])
                nc.scalar.copy(q_st[0][1][64:128, HALVES[half]], roped[64:128, HALVES[half]])\
                  .then_inc((first_hi_done, prod_hi_done)[half], 1)

            for c in range(KC):
                x_high(2, 0, c, c)
            act.wait_ge(down_done, 4)
            raw_half(0, 0, 0, 1.0, b=4)
            raw_half(1, 0, 1, Q_SCALE, b=5)
            v_high(0)
            v_high(1)
            for c in range(KC):
                x_high(2, 1, c, 2 + c)
            v_high(2)
            v_high(3)
            raw_half(0, 1, 2, 1.0, b=4)
            raw_half(1, 1, 3, Q_SCALE, b=5)
            v_high(4)
            k0_high(0)
            q0_high(0)
            v_high(5)
            v_high(6)
            k0_high(1)
            v_high(7)
            q0_high(1)

            def exp_unit(g, kind, k):
                p, i, a = unit(k)
                n = 32 * g + k
                width = (i + 1) * P
                act.wait_ge(nmax_done, n + 1)
                if not (kind == "first" and k < 2):
                    act.wait_ge(pT_done, 48 * g + chunks_to(k - 1))
                m = 2 * p + i // 4
                nc.scalar.activation(probs[k % 2][:, 0:width], PS[:, (k % 2) * 2 * BANK:(k % 2) * 2 * BANK + width],
                                     ACT.Exp, bias=nmax[:, k % 4:k % 4 + 1],
                                     accum_out=lsum[:, m % 2, (i % 4) * 2 + a:(i % 4) * 2 + a + 1])\
                  .then_inc(exp_done, 1)

            def evacuate_hi(g, kind, k):
                p, i, a = unit(k)
                half = i // 4
                s = 4 * g + (2 * p + half if k >= 0 else -1)
                for c in range(i // 4 + 1):
                    q = chunks_to(k) + c
                    j0, j1 = 4 * c, min(4 * c + 4, i + 1)
                    act.wait_ge(pT_done, 48 * g + q + 1)
                    if c == 0 and k % 8 < 2 and not (kind == "first" and 0 <= k < 16):
                        act.wait_ge(pv_done, s - 1)
                    dst = pT_hi[a][half][:, j0:j1, (i % 4) * P:(i % 4 + 1) * P]
                    nc.scalar.copy(dst, bank(4 + q % 2)[:, 0:(j1 - j0) * P].rearrange("p (j n) -> p j n", n=P))\
                      .then_inc(pT_hi_done, 1)

            def recip_out(g, kind, m, job):
                s = 4 * g + m
                act.wait_ge(misc_done, job + 1)
                if not (kind == "first" and m == 0):
                    act.wait_ge(o_done, s)
                nc.scalar.copy(recipT[:], bank(7)).then_inc(recipT_done, 1)

            def high_o(g, kind, m):
                s, mm = 4 * g + m, m % 4
                p, half = mm // 2, mm % 2
                act.wait_ge(o_done, s + 1)
                if m == 0 and kind != "first":
                    act.wait_ge(misc_done, misc_index(g, kind, "wo_3") + 1)
                nc.scalar.copy(oT_hi[:, p, half * BANK:(half + 1) * BANK], o32[:]).then_inc(o_hi_done, 1)

            def group(g, kind, par):
                for k in range(UNITS):
                    job = MISC.get(k - 1)
                    if job and has(kind, job):
                        index, last_char = misc_index(g, kind, job), int(job[-1])
                        if job[:2] == "f1":
                            raw_half(0, last_char, index, Q_SCALE, lambda: act.wait_ge(roped_done, 1))
                        elif job[:2] == "q1":
                            raw_half(1 - par, last_char, index, Q_SCALE,
                                     lambda: act.wait_ge(roped_done, 3 * g + 4))
                        elif job[:2] == "k_":
                            raw_half(1 - par, last_char, index, 1.0,
                                     lambda: act.wait_ge(q_landed[0], 32 * g + 32))
                        elif job[:2] == "q0":
                            raw_half(par, last_char, index, Q_SCALE,
                                     lambda: act.wait_ge(q_landed[1], 32 * g + 32))
                        elif job[:2] == "rl":
                            recip_out(g, kind, -1 if last_char == 3 else last_char, index)
                    if not (kind == "first" and k < LAG):
                        evacuate_hi(g, kind, k - LAG)
                    exp_unit(g, kind, k)
                    if k % 8 == AT["high_o"] and not (kind == "first" and k < 8):
                        high_o(g, kind, k // 8 - 1)

            run_groups(act, group)
            g = NG
            evacuate_hi(g, "mid", -2)
            evacuate_hi(g, "mid", -1)
            recip_out(g, "mid", -1, MISC_TAIL + 2)
            high_o(g, "mid", -1)

            def z_high(t):
                act.wait_ge(zT_done, t + 1)
                nc.scalar.copy(zT_hi[:, t % 2], bank(4, 2).rearrange("p (i n) -> p i n", i=NF)).then_inc(zT_hi_done, 1)

            def gelu_of(t):
                act.wait_ge(fc_done, t + 1)
                if t >= 2:
                    act.wait_ge(z_squares_done, t - 1)
                nc.scalar.activation(gelu[:, t % 2, :], bank(2 * (t % 2), 2), ACT.Gelu, scale=bit[:, 3, t:t + 1],
                                     accum_out=bit[:, 8, t:t + 1]).then_inc(gelu_done, 1)

            def centre(t):
                act.wait_ge(z_mean_done, t + 1)
                if t >= 2:
                    act.wait_ge(zT_done, t - 1)
                nc.scalar.activation(z[:, t % 2, :], gelu[:, t % 2, :], ACT.Identity,
                                     bias=bit[:, 9, t:t + 1]).then_inc(z_centred, 1)

            def squares(t):
                if t:
                    act.wait_ge(z_squares_done, t)
                nc.scalar.activation(square[:], gelu[:, t % 2, :], ACT.Square, bias=bit[:, 9, t:t + 1],
                                     accum_out=bit[:, 10, t:t + 1]).then_inc(z_squares_done, 1)

            for c in range(KC):
                x_high(3, 0, c, 4 + c)
            gelu_of(0)
            centre(0)
            for c in range(KC):
                x_high(3, 1, c, 6 + c)
            for t in range(NT):
                if t:
                    centre(t)
                if t + 1 < NT:
                    gelu_of(t + 1)
                if t:
                    z_high(t - 1)
                squares(t)
            z_high(NT - 1)

        @block.vector
        def _(dve):
            def tile_moments(st, i):
                nc.vector.bn_stats(stats[:, 6 * i:6 * i + 6], x[:, i, :]).then_inc(stats_done, 1)
                dve.wait_ge(stats_done, st * NT + i + 1)
                nc.vector.bn_aggr(moments[:, st, 2 * i:2 * i + 2], stats[:, 6 * i:6 * i + 6]).then_inc(moments_done, 1)

            def normalise(st, i):
                dve.wait_ge(rstd_done, st * NT + i + 1)
                nc.vector.tensor_scalar(xn[:, i, :], x[:, i, :], mean_of(st, i), moments[:, st, 2 * i + 1:2 * i + 2],
                                        ALU.subtract, ALU.mult).then_inc(xn_done, 1)

            def x_low(st, hf, c, b):
                dve.wait_ge(xT_hi_done, 4 * st + 2 * hf + c + 1)
                sl = slice(hf * BANK, (hf + 1) * BANK)
                nc.vector.tensor_tensor(xnT_lo[:, c, sl], bank(b), xnT_hi[:, c, sl].bitcast(F32),
                                        ALU.subtract).then_inc(xT_lo_done, 1)

            for i in range(NT):
                dve.wait_ge(x_landed[i // 2], 16)
                tile_moments(0, i)
                if i:
                    normalise(0, i - 1)
            normalise(0, NT - 1)
            for hf in range(2):
                for c in range(KC):
                    x_low(0, hf, c, 4 + 2 * hf + c)

            def w_low(k):
                dve.wait_ge(wT_hi_done, k + 1)
                if k < 8:
                    sl = slice((k // 2) * BANK, (k // 2 + 1) * BANK)
                    nc.vector.tensor_tensor(wguT_lo[:, k % 2, sl], bank(4 + k % 4), wguT_hi[:, k % 2, sl].bitcast(F32),
                                            ALU.subtract).then_inc(wT_lo_done, 1)
                else:
                    sl = slice(2 * (k - 8), 2 * (k - 7))
                    nc.vector.tensor_tensor(wdnT_lo[:, sl, :], bank(4 + k % 4).rearrange("p (i n) -> p i n", i=2),
                                            wdnT_hi[:, sl, :].bitcast(F32), ALU.subtract).then_inc(wT_lo_done, 1)

            dve.wait_ge(chain_pe, 2)
            nc.vector.tensor_copy(gram[:, 1, :], bank(1)[:, 0:C]).then_inc(chain_dve, 1)
            dve.wait_ge(chain_pe, 4)
            nc.vector.tensor_copy(gram_wk[:, 1, :], bank(3)[:, 0:C]).then_inc(chain_dve, 1)
            w_low(0)
            w_low(1)
            dve.wait_ge(chain_pe, 6)
            nc.vector.tensor_reduce(s_nmax, two_chunks(0), AX.X, ALU.max,
                                    negate=True).then_inc(soft_dve, 1)
            dve.wait_ge(soft_dve, 1)
            nc.vector.tensor_scalar(s_scaled, s_nmax, 8 ** -0.5, None, ALU.mult).then_inc(soft_dve, 1)
            dve.wait_ge(soft_act, 2)
            nc.vector.reciprocal(s_rec, s_sum).then_inc(soft_dve, 1)
            dve.wait_ge(soft_dve, 3)
            for m in range(KC):
                nc.vector.tensor_scalar(attn_a[:, m, :], attn_a[:, m, :], s_rec[:, m:m + 1], None,
                                        ALU.mult).then_inc(soft_dve, 1)
            for k in range(2, 6):
                w_low(k)
            dve.wait_ge(chain_pe, 8)
            nc.vector.tensor_copy(attn_wo[:, 1, :], bank(3)[:, 0:C]).then_inc(chain_dve, 1)
            w_low(6)
            w_low(7)
            dve.wait_ge(chain_act, 4)
            nc.vector.tensor_tensor(mix_lo[:], two_chunks(0), mix_hi[:].bitcast(F32),
                                    ALU.subtract).then_inc(chain_dve, 1)
            for k in range(8, 12):
                w_low(k)

            def add_pair(j, b, count):
                nc.vector.tensor_tensor(x[:, 2 * j:2 * j + 2, :], bank(b).rearrange("p (t n) -> p t n", t=2),
                                        x[:, 2 * j:2 * j + 2, :], ALU.add).then_inc(x_added, 1)
                dve.wait_ge(x_added, count)

            for j in range(4):
                dve.wait_ge(mixed_done, j + 1)
                add_pair(j, j, j + 1)
                for i in (2 * j, 2 * j + 1):
                    tile_moments(1, i)
                    if i:
                        normalise(1, i - 1)
            normalise(1, NT - 1)
            for hf in range(2):
                for c in range(KC):
                    x_low(1, hf, c, 4 + 2 * hf + c)

            def h_tile(n):
                dve.wait_ge(silu_done, n + 1)
                if n >= 3:
                    dve.wait_ge(h_lo_done, n - 2)
                nc.vector.tensor_tensor(h32[:, n % 3, :], silu[:, n % 2, :], bank(2 * (n % 2) + 1),
                                        ALU.mult).then_inc(h_done, 1)
                dve.wait_ge(h_done, n + 1)
                nc.vector.tensor_copy(hT_hi[:, n, :], h32[:, n % 3, :]).then_inc(h_hi_done, 1)

            def add_down(j):
                dve.wait_ge(down_done, j + 1)
                add_pair(j, 4 + j, 4 + j + 1)

            def ternary(m):
                nat = ((wfc_nat, wpj_nat)[m])[:].rearrange("p a b -> p (a b)")
                if m:
                    dve.wait_ge(tern_done, 1)
                nc.vector.tensor_scalar(above[:], nat, thr[:, m:m + 1], None, ALU.is_gt).then_inc(above_done, 1)
                dve.wait_ge(above_done, m + 1)
                nc.vector.scalar_tensor_tensor(out=tern[:, m, :], in0=nat, scalar=nthr[:, m:m + 1], in1=above[:],
                                               op0=ALU.is_lt, op1=ALU.subtract).then_inc(tern_done, 1)

            for n in range(2 * NF):
                h_tile(n)
                if n == 3:
                    dve.wait_ge(wv_landed, 16)
                    nc.vector.tensor_reduce(wv_max, wv_nat[:].rearrange("p c n -> p (c n)"), AX.X, ALU.max,
                                            apply_absolute_value=True).then_inc(wv_max_done, 1)
                if n == 8:
                    dve.wait_ge(wv_all_done, 1)
                    nc.vector.tensor_scalar(wv_max, wv_all, 1e-30, None, ALU.max).then_inc(v_scale_done, 1)
                    dve.wait_ge(v_scale_done, 1)
                    nc.vector.tensor_scalar(v_inv, wv_max, 1.0 / 128, None, ALU.mult).then_inc(v_scale_done, 1)
                    dve.wait_ge(v_scale_done, 2)
                    nc.vector.reciprocal(v_scale, v_inv).then_inc(v_scale_done, 1)
                    dve.wait_ge(gam_sum_done, 1)
                    nc.vector.tensor_scalar(gam, bank(4)[:, 0:2], 1.0 / (F * C), None, ALU.mult).then_inc(gam_done, 1)
                    dve.wait_ge(gam_done, 1)
                    nc.vector.tensor_scalar(thr, gam, BIT_EPS, 0.5, ALU.add, ALU.mult).then_inc(gam_done, 1)
                    nc.vector.tensor_scalar(ngam, gam, -1.0, None, ALU.mult).then_inc(gam_done, 1)
                    dve.wait_ge(gam_done, 3)
                    nc.vector.tensor_scalar(nthr, thr, -1.0, None, ALU.mult).then_inc(gam_done, 1)
                    dve.wait_ge(gam_done, 4)
                if n == 9:
                    ternary(0)
                if n == 10:
                    dve.wait_ge(wv_hi_done, 1)
                    nc.vector.tensor_tensor(wv_lo[:], wv_nat[:], wv_hi[:].bitcast(F32),
                                            ALU.subtract).then_inc(wv_lo_done, 1)
                if n == 11:
                    ternary(1)
                    add_down(0)
                    tile_moments(2, 0)
                    tile_moments(2, 1)
                if n == 13:
                    add_down(1)
                    tile_moments(2, 2)
                    tile_moments(2, 3)
                    normalise(2, 0)
                if n == 15:
                    normalise(2, 1)
                    normalise(2, 2)
                    normalise(2, 3)

            def v_low(t):
                dve.wait_ge(v_hi_done, t + 1)
                nc.vector.scalar_tensor_tensor(out=v_lo[:, t, :], in0=bank(V_BANK[t]), scalar=v_scale,
                                               in1=v_hi[:, t, :], op0=ALU.mult,
                                               op1=ALU.subtract).then_inc(v_lo_done, 1)

            add_down(2)
            tile_moments(2, 4)
            tile_moments(2, 5)
            x_low(2, 0, 0, 0)
            x_low(2, 0, 1, 1)
            normalise(2, 4)
            add_down(3)
            tile_moments(2, 6)
            tile_moments(2, 7)
            normalise(2, 5)
            normalise(2, 6)
            normalise(2, 7)
            v_low(0)
            v_low(1)
            for c in range(KC):
                x_low(2, 1, c, 2 + c)
            def k0_rope(half):
                tok = HALVES[half]
                dve.wait_ge(raw_done, 2 * half + 1)
                nc.vector.tensor_tensor(k0_roped[:, tok], raw[0][:, tok], cosT[:, tok], ALU.mult).then_inc(k0_mul, 1)
                dve.wait_ge(k0_swap_landed[half], 64)
                nc.vector.tensor_tensor(k0_swapped[:, tok], k0_swapped[:, tok], sinT[:, tok],
                                        ALU.mult).then_inc(k0_mul, 1)
                dve.wait_ge(k0_mul, 2 * half + 2)
                nc.vector.tensor_tensor(k0_roped[:, tok], k0_roped[:, tok], k0_swapped[:, tok],
                                        ALU.add).then_inc((k0_roped_done, roped_done)[half], 1)

            def k0_low(half):
                tok = HALVES[half]
                dve.wait_ge((first_hi_done, prod_hi_done)[half], 1)
                nc.vector.tensor_tensor(k_ll[0][:, tok], k0_roped[:, tok], k_hh[0][:, tok].bitcast(F32),
                                        ALU.subtract).then_inc((k0_lo_done, prod_lo_done)[half], 1)

            dve.wait_ge(rope_landed, 32)
            v_low(2)
            k0_rope(0)
            v_low(3)
            v_low(4)
            k0_low(0)
            k0_rope(1)
            v_low(5)
            v_low(6)
            k0_low(1)
            v_low(7)
            for q in range(4):
                dve.wait_ge(ternT_done, q + 1)
                src = bank(4 + q).bitcast(F16)
                if q < 2:
                    nc.vector.tensor_copy(fcT[:, q, :], src).then_inc(ternT_kept, 1)
                else:
                    nc.vector.tensor_copy(pjT[:, 4 * (q - 2):4 * (q - 1), :],
                                          src.rearrange("p (i n) -> p i n", i=4)).then_inc(ternT_kept, 1)

            def row_max(g, kind, k):
                p, i, a = unit(k)
                dve.wait_ge(scores_done, 32 * g + k + 1)
                nc.vector.tensor_reduce(nmax[:, k % 4:k % 4 + 1],
                                        PS[:, (k % 2) * 2 * BANK:(k % 2) * 2 * BANK + (i + 1) * P], AX.X, ALU.max,
                                        negate=True).then_inc(nmax_done, 1)

            def evacuate_lo(g, k):
                p, i, a = unit(k)
                half = i // 4
                for c in range(i // 4 + 1):
                    q = chunks_to(k) + c
                    j0, j1 = 4 * c, min(4 * c + 4, i + 1)
                    sl = (slice(None), slice(j0, j1), slice((i % 4) * P, (i % 4 + 1) * P))
                    dve.wait_ge(pT_hi_done, 48 * g + q + 1)
                    nc.vector.tensor_tensor(pT_lo[a][half][sl],
                                            bank(4 + q % 2)[:, 0:(j1 - j0) * P].rearrange("p (j n) -> p j n", n=P),
                                            pT_hi[a][half][sl], ALU.subtract).then_inc(pT_lo_done, 1)

            def recips(g, kind, m, used=None):
                s, b = 4 * g + m, m % 2
                if m == -1:
                    dve.wait_ge(exp_done, 32 * g)
                else:
                    dve.wait_ge(exp_done, 32 * g + 8 * m + 8)
                nc.vector.reciprocal(lrec[:, b, :], lsum[:, b, :]).then_inc(recip_done, 1)
                dve.wait_ge(recip_done, s + 1)
                if m == -1:
                    dve.wait_ge(misc_done, misc_before(g, kind) if used is None else used)
                elif m > 0:
                    dve.wait_ge(misc_done, misc_index(g, kind, f"rl{m - 1}") + 1)
                elif kind != "first":
                    dve.wait_ge(misc_done, misc_index(g, kind, "rl3") + 1)
                nc.vector.tensor_scalar(recip_b[:].rearrange("p i (a d) -> p (i a) d", a=2),
                                        lrec[:, b, :].unsqueeze(2).broadcast_to([P, 8, HEAD]), v_inv, None,
                                        ALU.mult).then_inc(recip_b_done, 1)

            def scale_o(g, kind, m):
                s = 4 * g + m
                dve.wait_ge(pv_done, s + 1)
                dve.wait_ge(recipT_done, s + 1)
                if not (kind == "first" and m == 0):
                    dve.wait_ge(o_lo_done, s)
                nc.vector.tensor_tensor(o32[:], bank(6), recipT[:], ALU.mult).then_inc(o_done, 1)

            def split(nat, hi, lo, landed, value, used, done, count):
                dve.wait_ge(landed, value)
                dve.wait_ge(misc_done, used)
                nc.vector.tensor_copy(hi[:], nat[:]).then_inc(split_hi, 1)
                dve.wait_ge(split_hi, count)
                nc.vector.tensor_tensor(lo[:], nat[:], hi[:].bitcast(F32), ALU.subtract).then_inc(done, 1)

            def high_q(r, p):
                dve.wait_ge(roped_done, r + 1)
                nc.vector.tensor_copy(q_st[p][0][0:64, :], roped[0:64, :])
                nc.vector.tensor_copy(q_st[p][1][64:128, :], roped[64:128, :]).then_inc(prod_hi_done, 1)

            def high_k(r, slot):
                dve.wait_ge(roped_done, r + 1)
                nc.vector.tensor_copy(k_hh[slot][:], roped[:]).then_inc(prod_hi_done, 1)

            def splits_before(g, kind):
                return 3 if kind == "first" else 3 + 3 + 4 * (g - 1)

            def group(g, kind, par):
                n_split = splits_before(g, kind)
                at = [0]

                def next_split():
                    at[0] += 1
                    return n_split + at[0]

                for k in range(UNITS):
                    job = MISC.get(k - 1)
                    if job and has(kind, job) and job[:2] == "wo":
                        j = int(job[-1])
                        dve.wait_ge(misc_done, misc_index(g, kind, job) + 1)
                        nc.vector.tensor_tensor(x[:, 2 * j:2 * j + 2, :], bank(7).rearrange("p (t n) -> p t n", t=2),
                                                x[:, 2 * j:2 * j + 2, :], ALU.add).then_inc(x_added, 1)
                    row_max(g, kind, k)
                    if k % 8 == AT["scale_o"] and not (kind == "first" and k < 8):
                        scale_o(g, kind, k // 8 - 1)
                    if k % 8 == AT["recips"] and not (kind == "first" and k < 8):
                        recips(g, kind, k // 8 - 1)
                    if not (kind == "first" and k < LAG):
                        evacuate_lo(g, k - LAG)
                    if k == AT["high_f1" if kind == "first" else "high_q1"]:
                        high_q(3 * g + 2, 1)
                    if k == AT["high_k"] and kind != "last":
                        high_k(3 * g + 3, 1 - par)
                    if k == AT["high_q0"] and kind != "last":
                        high_q(3 * g + 4, 0)
                    if k == AT["split_wk"] and kind != "last":
                        split(wk_nat, wk_hi, wk_lo, wk_landed, 32 * g + 64, misc_before(g, kind), wk_split,
                              next_split())
                    if k == AT["values"]:
                        if kind != "first":
                            dve.wait_ge(pv_done, 4 * g)
                        nc.vector.tensor_copy(vg_hi[:], v_hi[:, :, bass.ds(g * HEAD, HEAD)])
                        nc.vector.tensor_copy(vg_lo[:], v_lo[:, :, bass.ds(g * HEAD, HEAD)]).then_inc(vg_done, 1)
                    if k == AT["split_wo"] and kind != "first":
                        split(wo_nat, wo_hi, wo_lo, wo_landed, 32 * g, misc_before(g, kind), wo_split, next_split())
                    if k == AT["split_wq0"] and kind != "last":
                        split(wq_nat[0], wq_hi[0], wq_lo[0], wq_landed[0], 16 * g + 32, misc_before(g, kind),
                              wq_split[0], next_split())
                    if k == 20 and kind == "last":
                        split(wo_nat, wo_hi, wo_lo, wo_landed, 32 * NG, misc_index(g, kind, "wo_3") + 1, wo_split,
                              next_split())
                    if k == AT["split_wq1"] and kind != "last":
                        split(wq_nat[1], wq_hi[1], wq_lo[1], wq_landed[1], 16 * g + 32,
                              misc_index(g, kind, "f1_1") + 1 if kind == "first" else misc_before(g, kind),
                              wq_split[1], next_split())

            run_groups(dve, group)
            g = NG
            evacuate_lo(g, -2)
            evacuate_lo(g, -1)
            recips(g, "mid", -1, MISC_TAIL)

            ADDS = 8 + 4 * (NG - 1)
            steps = [0]

            def step(ins):
                steps[0] += 1
                ins.then_inc(bit_step, 1)
                dve.wait_ge(bit_step, steps[0])

            def add_last(j, job):
                dve.wait_ge(misc_done, job + 1)
                if j == 0:
                    dve.wait_ge(x_added, ADDS)
                add_pair(j, j, ADDS + j + 1)
                for i in (2 * j, 2 * j + 1):
                    tile_moments(3, i)

            rstds = moments[:, 3, :].rearrange("p (i two) -> p i two", two=2)

            def quantise(hf):
                tiles = slice(4 * hf, 4 * hf + 4)
                dve.wait_ge(moments_done, 3 * NT + 4 * hf + 4)
                for i in range(4 * hf, 4 * hf + 4):
                    last = nc.vector.tensor_scalar(y[:, i, :], x[:, i, :], mean_of(3, i), None, ALU.subtract)
                    if i < 4 * hf + 3:
                        steps[0] += 1
                        last.then_inc(bit_step, 1)
                step(last)
                step(nc.vector.tensor_reduce(bit[:, 0, tiles], y[:, tiles, :], AX.X, ALU.max,
                                             apply_absolute_value=True))
                step(nc.vector.tensor_scalar(bit[:, 1, tiles], bit[:, 0, tiles], 1.0 / Q_B, None, ALU.mult))
                step(nc.vector.reciprocal(bit[:, 2, tiles], bit[:, 1, tiles]))
                for i in range(4 * hf, 4 * hf + 4):
                    nc.vector.tensor_scalar(y[:, i, :], y[:, i, :], bit[:, 2, i:i + 1], Q_B, ALU.mult,
                                            ALU.min).then_inc(y_done, 1)
                dve.wait_ge(rstd_done, 3 * NT + 4 * hf + 4)
                nc.vector.scalar_tensor_tensor(out=bit[:, 3, tiles], in0=bit[:, 1, tiles], scalar=ngam[:, 0:1],
                                               in1=rstds[:, tiles, 1], op0=ALU.mult, op1=ALU.mult)

            def y_low(hf):
                for c in range(KC):
                    dve.wait_ge(xT_hi_done, 12 + 2 * hf + c + 1)
                    sl = slice(hf * BANK, (hf + 1) * BANK)
                    nc.vector.scalar_tensor_tensor(out=yT_lo[:, c, sl], in0=bank(4 + 2 * hf + c), scalar=-Q_B,
                                                   in1=yT_hi[:, c, sl], op0=ALU.max,
                                                   op1=ALU.subtract).then_inc(xT_lo_done, 1)

            add_last(0, MISC_TAIL)
            add_last(1, MISC_TAIL + 1)
            scale_o(g, "mid", -1)
            quantise(0)
            add_last(2, MISC_TAIL + 3)
            y_low(0)
            add_last(3, MISC_TAIL + 4)
            quantise(1)
            y_low(1)

            def z_low(t):
                dve.wait_ge(zT_hi_done, t + 1)
                nc.vector.scalar_tensor_tensor(out=zT_lo[:, t % 2], in0=bank(4, 2).rearrange("p (i n) -> p i n", i=NF),
                                               scalar=-Q_B, in1=zT_hi[:, t % 2], op0=ALU.max,
                                               op1=ALU.subtract).then_inc(zT_lo_done, 1)

            def result(t):
                dve.wait_ge(z_rstd_done, t + 1)
                step(nc.vector.tensor_scalar(bit[:, 7, t:t + 1], bit[:, 5, t:t + 1], bit[:, 10, t:t + 1],
                                             ngam[:, 1:2], ALU.mult, ALU.mult))
                dve.wait_ge(pj_done, t + 1)
                nc.vector.scalar_tensor_tensor(out=x[:, t, :], in0=bank(6 + t % 2)[:, 0:C], scalar=bit[:, 7, t:t + 1],
                                               in1=x[:, t, :], op0=ALU.mult, op1=ALU.add).then_inc(result_done, 1)

            for t in range(NT):
                dve.wait_ge(z_centred, t + 1)
                step(nc.vector.tensor_reduce(bit[:, 4, t:t + 1], z[:, t % 2, :], AX.X, ALU.max,
                                             apply_absolute_value=True))
                step(nc.vector.tensor_scalar(bit[:, 5, t:t + 1], bit[:, 4, t:t + 1], 1.0 / Q_B, None, ALU.mult))
                step(nc.vector.reciprocal(bit[:, 6, t:t + 1], bit[:, 5, t:t + 1]))
                nc.vector.tensor_scalar(z[:, t % 2, :], z[:, t % 2, :], bit[:, 6, t:t + 1], Q_B, ALU.mult,
                                        ALU.min).then_inc(z_done, 1)
                if t >= 1:
                    z_low(t - 1)
                if t >= 2:
                    result(t - 2)
            z_low(NT - 1)
            result(NT - 2)
            result(NT - 1)

        @block.tensor
        def _(pe):
            def product(dst, pairs):
                for n, (lhsT, rhs) in enumerate(pairs):
                    last = nc.tensor.matmul(dst, lhsT, rhs, start=n == 0, stop=n == len(pairs) - 1)
                return last

            def three(lhs, rhs):
                return [(lhs[0], rhs[0]), (lhs[1], rhs[0]), (lhs[0], rhs[1])]

            def x_transposes(st, hf, first_bank):
                src = y if st == 3 else xn
                for c in range(KC):
                    for q in range(4):
                        i = 4 * hf + q
                        if c == 0:
                            pe.wait_ge(y_done if st == 3 else xn_done, (0 if st == 3 else st * NT) + i + 1)
                        last = nc.tensor.transpose(bank(first_bank + 2 * hf + c)[:, q * P:(q + 1) * P],
                                                   src[:, i, c * P:(c + 1) * P], identf[:])
                    last.then_inc(xT_done, 1)

            pe.wait_ge(const_ready, 1)
            pe.wait_ge(wa_landed[2], 16)
            for f in range(KC):
                for c in range(KC):
                    last = nc.tensor.transpose(bank(2)[:, f * C + c * P:f * C + (c + 1) * P],
                                               wv_a_sb[:, c, f * P:(f + 1) * P], identf[:])
            last.then_inc(wvT_done, 1)
            for hf in range(2):
                x_transposes(0, hf, 4)
            for m in range(KC):
                product(bank(m)[:, 0:C], [(xn[:, i, m * P:(m + 1) * P], xn[:, i, :]) for i in range(NT)])\
                    .then_inc(chain_pe, 1)

            def w_transposes(k):
                if k == 0:
                    pe.wait_ge(wgu_landed[0], 16)
                if k == 4:
                    pe.wait_ge(wgu_landed[1], 16)
                if k == 8:
                    pe.wait_ge(wdn_landed, 16)
                if k < 4:
                    pe.wait_ge(xT_lo_done, k + 1)
                else:
                    pe.wait_ge(wT_lo_done, k - 3)
                for q in range(4):
                    src = wgu_nat[:, 4 * (k // 2) + q, (k % 2) * P:(k % 2 + 1) * P] if k < 8 else \
                        wdn_nat[:, q % 2, (2 * (k - 8) + q // 2) * P:(2 * (k - 8) + q // 2 + 1) * P]
                    last = nc.tensor.transpose(bank(4 + k % 4)[:, q * P:(q + 1) * P], src, identf[:])
                last.then_inc(wT_done, 1)

            def chain(dst_bank, lhs, rhs):
                for m in range(KC):
                    product(bank(dst_bank + m)[:, 0:C],
                            [(lhs[:, c, m * P:(m + 1) * P], rhs[:, c, :]) for c in range(KC)]).then_inc(chain_pe, 1)

            pe.wait_ge(chain_act, 1)
            pe.wait_ge(chain_dve, 1)
            pe.wait_ge(wvT_kept, 1)
            pe.wait_ge(wa_landed[0], 16)
            chain(2, gram, wk_a_sb)
            w_transposes(0)
            w_transposes(1)
            pe.wait_ge(chain_act, 2)
            pe.wait_ge(chain_dve, 2)
            pe.wait_ge(wa_landed[1], 16)
            chain(0, wq_a_sb, gram_wk)
            for k in range(2, 6):
                w_transposes(k)
            pe.wait_ge(soft_dve, 5)
            pe.wait_ge(wa_landed[3], 16)
            chain(2, attn_a, wo_a_sb)
            w_transposes(6)
            w_transposes(7)
            pe.wait_ge(chain_act, 3)
            pe.wait_ge(chain_dve, 3)
            chain(0, wvT_a, attn_wo)
            for k in range(8, 12):
                w_transposes(k)
            pe.wait_ge(chain_act, 4)
            pe.wait_ge(chain_dve, 4)
            for j in range(4):
                for t in (2 * j, 2 * j + 1):
                    tok = slice(t * P, (t + 1) * P)
                    last = product(bank(j)[:, (t % 2) * C:(t % 2 + 1) * C],
                                   [pr for c in range(KC) for pr in
                                    three((xnT_hi[:, c, tok], xnT_lo[:, c, tok]), (mix_hi[:, c, :], mix_lo[:, c, :]))])
                last.then_inc(mixed_done, 1)

            pe.wait_ge(wT_lo_done, 12)
            for hf in range(2):
                x_transposes(1, hf, 4)

            def gate_up(n):
                hf, ft = n // NF, n % NF
                if ft == 0:
                    pe.wait_ge(xT_lo_done, 4 + 2 * hf + 2)
                if n >= 2:
                    pe.wait_ge(h_done, n - 1)
                if n == 0:
                    pe.wait_ge(x_added, 4)
                tok = slice(hf * BANK, (hf + 1) * BANK)
                for half in range(2):
                    ft_s = slice(half * F + ft * P, half * F + (ft + 1) * P)
                    last = product(bank(2 * (n % 2) + half),
                                   [pr for c in range(KC) for pr in
                                    three((wguT_hi[:, c, ft_s], wguT_lo[:, c, ft_s]),
                                          (xnT_hi[:, c, tok], xnT_lo[:, c, tok]))])
                last.then_inc(gate_up_done, 1)

            def down(j):
                hf = j // 2
                pe.wait_ge(h_lo_done, NF * (hf + 1))
                if j == 0:
                    pe.wait_ge(gam_done, 1)
                for t in (2 * j, 2 * j + 1):
                    tok = slice((t % 4) * P, (t % 4 + 1) * P)
                    last = product(bank(4 + j)[:, (t % 2) * C:(t % 2 + 1) * C],
                                   [pr for i in range(NF) for pr in
                                    three((hT_hi[:, hf * NF + i, tok], hT_lo[:, hf * NF + i, tok]),
                                          (wdnT_hi[:, i, :], wdnT_lo[:, i, :]))])
                last.then_inc(down_done, 1)

            for n in range(2 * NF):
                gate_up(n)
                if n == 8:
                    pe.wait_ge(abs_done, 2)
                    nc.tensor.matmul(bank(4)[:, 0:2], ones[:], abs_sum, start=True, stop=True)\
                      .then_inc(gam_sum_done, 1)
                if n == 10:
                    down(0)
                if n == 12:
                    down(1)
            down(2)
            x_transposes(2, 0, 0)
            down(3)

            def project(split_done, value, hi, lo, half, b=7):
                pe.wait_ge(split_done, value)
                tok = slice(half * BANK, (half + 1) * BANK)
                product(bank(b), [pr for c in range(KC) for pr in
                                  three((hi[:, c, :], lo[:, c, :]), (xnT_hi[:, c, tok], xnT_lo[:, c, tok]))])\
                    .then_inc(misc_done, 1)

            def values(t):
                tok = slice(t * P, (t + 1) * P)
                product(bank(V_BANK[t]), [pr for c in range(KC) for pr in
                                          three((xnT_hi[:, c, tok], xnT_lo[:, c, tok]),
                                                (wv_hi[:, c, :], wv_lo[:, c, :]))]).then_inc(v_done, 1)

            pe.wait_ge(xT_lo_done, 10)
            project(wk_split, 1, wk0_hi, wk0_lo, 0, 4)
            project(wq_split[0], 1, wq0_hi, wq0_lo, 0, 5)
            pe.wait_ge(wv_lo_done, 1)
            values(0)
            values(1)
            x_transposes(2, 1, 0)
            values(2)
            values(3)
            pe.wait_ge(xT_lo_done, 12)
            pe.wait_ge(raw_done, 1)
            project(wk_split, 1, wk0_hi, wk0_lo, 1, 4)
            pe.wait_ge(raw_done, 2)
            project(wq_split[0], 1, wq0_hi, wq0_lo, 1, 5)
            pe.wait_ge(v_lo_done, 2)
            for t in range(4, NT):
                values(t)
            pe.wait_ge(tern_done, 2)
            pe.wait_ge(raw_done, 4)
            for q in range(4):
                if q == 2:
                    pe.wait_ge(v_lo_done, 4)
                dst = bank(4 + q).bitcast(F16)
                for b in range(8):
                    src = tern[:, 0, b * C + q * P:b * C + (q + 1) * P] if q < 2 else \
                        tern[:, 1, (b % 2) * F + (4 * (q - 2) + b // 2) * P:(b % 2) * F + (4 * (q - 2) + b // 2 + 1) * P]
                    last = nc.tensor.transpose(dst[:, b * P:(b + 1) * P], src, identh[:])
                last.then_inc(ternT_done, 1)
            pe.wait_ge(v_lo_done, NT)

            def scores(g, kind, k, par):
                p, i, a = unit(k)
                n = 32 * g + k
                if k == 0 and kind == "first":
                    pe.wait_ge(k0_lo_done, 1)
                    pe.wait_ge(q0_landed, 32)
                    pe.wait_ge(first_hi_done, 2)
                if k == (8 if kind == "first" else 0):
                    pe.wait_ge(prod_lo_done, 3 * g + 1)
                    pe.wait_ge(q_landed[0], 32 * g + 32)
                    pe.wait_ge(prod_hi_done, 3 * g + 2)
                if k == 16:
                    pe.wait_ge(q_landed[1], 32 * g + 32)
                    pe.wait_ge(prod_hi_done, 3 * g + 3)
                if not (kind == "first" and k < 2):
                    pe.wait_ge(exp_done, n - 1)
                q = q_st[p][a][:, i * P:(i + 1) * P]
                width = (i + 1) * P
                for c0 in range(0, width, BANK):
                    w = min(width - c0, BANK)
                    cols = slice(c0, c0 + max(w, 256))
                    dst = bank((k % 2) * 2 + c0 // BANK)[:, 0:max(w, 256)]
                    nc.tensor.matmul(dst, q, k_hh[par][:, cols], start=True, stop=False)
                    if c0 + w == width:
                        nc.tensor.matmul(dst[:, w - P:w], identb[:], maskb[:], start=False, stop=False,
                                         skip_group_check=True)
                    last = nc.tensor.matmul(dst, q, k_ll[par][:, cols], start=False, stop=True)
                last.then_inc(scores_done, 1)

            def probs_transposes(g, kind, k):
                p, i, a = unit(k)
                pe.wait_ge(exp_done, 32 * g + k + 1)
                for c in range(i // 4 + 1):
                    q = chunks_to(k) + c
                    if not (kind == "first" and q in (0, 1)):
                        pe.wait_ge(pT_lo_done, 48 * g + q - 1)
                    for j in range(4 * c, min(4 * c + 4, i + 1)):
                        last = nc.tensor.transpose(bank(4 + q % 2)[:, (j % 4) * P:(j % 4 + 1) * P],
                                                   probs[k % 2][:, j * P:(j + 1) * P], identf[:])
                    last.then_inc(pT_done, 1)

            def pv(g, kind, m, piece):
                s, half = 4 * g + m, m % 2
                last_j = 4 * half + 3
                if piece == 0:
                    pe.wait_ge(pT_lo_done, 48 * g + chunks_to(8 * m + 8))
                    if m == -1:
                        pe.wait_ge(vg_done, g)
                    else:
                        pe.wait_ge(vg_done, g + 1)
                    if not (kind == "first" and m == 0):
                        pe.wait_ge(o_done, s)
                def passes(j, parts):
                    off = max(0, j - 4 * half) * P
                    for v, pt, start, stop in parts:
                        for a in range(2):
                            last = nc.tensor.matmul(bank(6)[64 * a:64 * a + 64, off:BANK], v[:, j, :],
                                                    pt[a][half][:, j, off:BANK], start=start, stop=stop,
                                                    skip_group_check=True)
                    return last
                for j in (2 * piece, 2 * piece + 1):
                    parts = [(vg_hi, pT_hi, j == 0, False), (vg_hi, pT_lo, False, False)]
                    if j:
                        parts.append((vg_lo, pT_hi, False, False))
                    passes(j, parts)
                if 2 * piece + 1 == last_j:
                    passes(0, [(vg_lo, pT_hi, False, True)]).then_inc(pv_done, 1)

            def misc_emptied(g, kind, name):
                half_or_m = int(name[-1])
                if name[:2] == "f1":
                    pe.wait_ge(raw_done, 5 + half_or_m)
                elif name[:2] == "q1":
                    pe.wait_ge(raw_done, 6 * g + 11 + half_or_m)
                elif name[:2] == "k_":
                    pe.wait_ge(raw_done, 6 * g + 7 + half_or_m)
                elif name[:2] == "q0":
                    pe.wait_ge(raw_done, 6 * g + 9 + half_or_m)
                elif name[:2] == "wo":
                    pe.wait_ge(x_added, 8 + 4 * (g - 1) + half_or_m + 1)
                else:
                    pe.wait_ge(recipT_done, 4 * g + (half_or_m + 1) % 4)

            def misc_free(g, kind, name):
                before = jobs(kind).index(name) - 1
                if before >= 0:
                    misc_emptied(g, kind, jobs(kind)[before])
                elif kind == "first":
                    pe.wait_ge(ternT_kept, 4)
                else:
                    misc_emptied(g - 1, "mid", jobs("mid")[-1])

            def recip_transposes(s):
                pe.wait_ge(recip_b_done, s + 1)
                for i in range(4):
                    last = nc.tensor.transpose(bank(7)[:, i * P:(i + 1) * P], recip_b[:, i, :], identf[:])
                last.then_inc(misc_done, 1)

            def out_project(g, j, b=7):
                if j == 0 and b == 7:
                    pe.wait_ge(o_lo_done, 4 * g + 4)
                    pe.wait_ge(wo_split, g + 1)
                for t in (2 * j, 2 * j + 1):
                    tok = slice(t * P, (t + 1) * P)
                    last = product(bank(b)[:, (t % 2) * C:(t % 2 + 1) * C],
                                   [pr for p in range(2) for pr in
                                    three((oT_hi[:, p, tok], oT_lo[:, p, tok]), (wo_hi[:, p, :], wo_lo[:, p, :]))])
                last.then_inc(misc_done, 1)

            def group(g, kind, par):
                for k in range(UNITS):
                    scores(g, kind, k, par)
                    if not (kind == "first" and k < LAG):
                        probs_transposes(g, kind, k - LAG)
                    piece, m = k % 8 - AT["pv"], k // 8 - 1
                    if 0 <= piece < 2 + 2 * (m % 2) and not (kind == "first" and m == -1):
                        pv(g, kind, m, piece)
                    job = MISC.get(k)
                    if job and has(kind, job):
                        misc_free(g, kind, job)
                        last_char = int(job[-1])
                        if job[:2] == "f1":
                            project(wq_split[1], 1, wq_hi[1], wq_lo[1], last_char)
                        elif job[:2] == "q1":
                            project(wq_split[1], g + 2, wq_hi[1], wq_lo[1], last_char)
                        elif job[:2] == "k_":
                            project(wk_split, g + 2, wk_hi, wk_lo, last_char)
                        elif job[:2] == "q0":
                            project(wq_split[0], g + 2, wq_hi[0], wq_lo[0], last_char)
                        elif job[:2] == "wo":
                            out_project(g - 1, last_char)
                        else:
                            recip_transposes(4 * g + (-1 if last_char == 3 else last_char))

            run_groups(pe, group)
            g = NG
            probs_transposes(g, "mid", -2)
            probs_transposes(g, "mid", -1)
            pe.wait_ge(o_lo_done, 4 * NG - 1)
            pe.wait_ge(wo_split, NG)
            out_project(NG - 1, 0, 0)
            out_project(NG - 1, 1, 1)
            pe.wait_ge(recipT_done, 4 * NG - 1)
            recip_transposes(4 * NG - 1)
            for piece in range(4):
                pv(g, "mid", -1, piece)
            pe.wait_ge(o_lo_done, 4 * NG)
            out_project(NG - 1, 2, 2)
            out_project(NG - 1, 3, 3)

            x_transposes(3, 0, 4)

            def fc(t):
                if t >= 2:
                    pe.wait_ge(gelu_done, t - 1)
                elif t == 1:
                    pe.wait_ge(x_added, 8 + 4 * NG)
                pe.wait_ge(xT_lo_done, 14 if t < 4 else 16)
                tok = slice(t * P, (t + 1) * P)
                for n in range(2):
                    cols = slice(n * BANK, (n + 1) * BANK)
                    last = product(bank(2 * (t % 2) + n), [(yT[:, c, tok], fcT[:, c, cols])
                                                           for c in range(KC) for yT in (yT_hi, yT_lo)])
                last.then_inc(fc_done, 1)

            def z_transposes(t):
                pe.wait_ge(z_done, t + 1)
                if t >= 1:
                    pe.wait_ge(zT_lo_done, t)
                for i in range(NF):
                    last = nc.tensor.transpose(bank(4, 2)[:, i * P:(i + 1) * P], z[:, t % 2, i * P:(i + 1) * P],
                                               identf[:])
                last.then_inc(zT_done, 1)

            def pj(t):
                pe.wait_ge(zT_lo_done, t + 1)
                if t == 0:
                    pe.wait_ge(xT_lo_done, 16)
                if t >= 2:
                    pe.wait_ge(result_done, t - 1)
                product(bank(6 + t % 2)[:, 0:C], [(zT[:, t % 2, i, :], pjT[:, i, :])
                                                  for i in range(NF) for zT in (zT_hi, zT_lo)]).then_inc(pj_done, 1)

            fc(0)
            fc(1)
            x_transposes(3, 1, 4)
            for t in range(NT):
                if t + 2 < NT:
                    fc(t + 2)
                z_transposes(t)
                if t >= 1:
                    pj(t - 1)
            pj(NT - 1)


_INS = ["L0_attn_x", "L0_attn_Wq", "L0_attn_Wk", "L0_attn_Wv", "L0_attn_Wo", "L0_ffn_w_gate_up", "L0_ffn_w_down",
        "L1_attn_wq", "L1_attn_wk", "L1_attn_wv", "L1_attn_wo", "L1_ffn_w_fc", "L1_ffn_w_proj"]


def rope_tables(tokens, head, heads):
    import numpy as np

    freqs = (np.float32(10000.0) ** (-np.arange(0, head, 2, dtype=np.float32) / np.float32(head))).astype(np.float32)
    theta = np.outer(freqs, np.arange(tokens, dtype=np.float32)).astype(np.float32)
    cos = np.cos(theta).astype(np.float32)
    sin = np.sin(theta).astype(np.float32)
    return (np.ascontiguousarray(np.concatenate([cos, cos] * heads)),
            np.ascontiguousarray(np.concatenate([-sin, sin] * heads)))


def kernel(**inputs):
    import numpy as np
    import concourse.bacc as bacc
    from concourse import mybir as _mybir
    from concourse.bass_utils import run_bass_kernel_spmd

    nc = bacc.Bacc("TRN2", target_bir_lowering=False, num_devices=1)
    cos, sin = rope_tables(1024, 64, 2)
    arrays = {name: np.ascontiguousarray(inputs[name]) for name in _INS}
    arrays["rope_cos"], arrays["rope_sin"] = cos, sin
    args = [nc.dram_tensor(n, a.shape, _mybir.dt.from_np(a.dtype), kind="ExternalInput").ap() for n, a in arrays.items()]
    out = nc.dram_tensor("out_0", (1, 1024, 256), F32, kind="ExternalOutput").ap()
    transformer_program(nc, *args, out)
    r = run_bass_kernel_spmd(nc, [arrays], core_ids=[0])
    return r.results[0]["out_0"]
```
